# Optimizing a Trainium2 kernel written in Bass

```python
import numpy as np
import jax
import jax.numpy as jnp

def _softmax(x, axis=-1):
    return jax.nn.softmax(x, axis=axis)

def _gelu(x):
    return jax.nn.gelu(x, approximate=True)

def _silu(x):
    return jax.nn.silu(x)

def _sigmoid(x):
    return jax.nn.sigmoid(x)

def _layernorm(x, axis=-1, eps=1e-05):
    m = jnp.mean(x, axis=axis, keepdims=True)
    v = jnp.var(x, axis=axis, keepdims=True)
    return (x - m) / jnp.sqrt(v + eps)

def _scatter_add(tgt, idx, src, axis=0):
    return tgt.at[idx].add(src)

def _segment_sum(src, seg, n):
    return jax.ops.segment_sum(src, seg, n)
kernel_name = 'mk_prb_d1_jaxref_r4_85c1eb'

def setup_inputs(seed: int=0):
    np.random.seed(seed)
    _w = jnp.asarray

    def _L0_attn_setup():
        import jax, jax.numpy as jnp
        import numpy as np
        D_MODEL = 512
        D_STATE = 128
        HEADDIM = 64
        EXPAND = 2
        D_CONV = 4
        NGROUPS = 1
        CHUNK = 64
        EPS = 1e-05
        D_INNER = EXPAND * D_MODEL
        NHEADS = D_INNER // HEADDIM
        CONV_DIM = D_INNER + 2 * NGROUPS * D_STATE
        D_IN_PROJ = 2 * D_INNER + 2 * NGROUPS * D_STATE + NHEADS

        def _segsum(a):
            T = a.shape[-1]
            cs = jnp.cumsum(a, axis=-1)
            d = cs[..., :, None] - cs[..., None, :]
            mask = jnp.tril(jnp.ones((T, T), dtype=bool))
            return jnp.where(mask, d, -jnp.inf)

        def _ssd(X, A, Bm, Cm):
            b, l, h, p = X.shape
            n = Bm.shape[-1]
            c = l // CHUNK
            X = X.reshape(b, c, CHUNK, h, p)
            A = A.reshape(b, c, CHUNK, h).transpose(0, 3, 1, 2)
            Bm = Bm.reshape(b, c, CHUNK, n)
            Cm = Cm.reshape(b, c, CHUNK, n)
            A_cs = jnp.cumsum(A, axis=-1)
            Lmat = jnp.exp(_segsum(A))
            Y_diag = jnp.einsum('bcln,bcsn,bhcls,bcshp->bclhp', Cm, Bm, Lmat, X)
            decay_states = jnp.exp(A_cs[..., -1:] - A_cs)
            states = jnp.einsum('bcln,bhcl,bclhp->bchpn', Bm, decay_states, X)
            A_last = jnp.pad(A_cs[..., -1], ((0, 0), (0, 0), (1, 0)))
            decay_chunk = jnp.exp(_segsum(A_last))
            states = jnp.concatenate([jnp.zeros_like(states[:, :1]), states], axis=1)
            states = jnp.einsum('bhzc,bchpn->bzhpn', decay_chunk, states)[:, :-1]
            Y_off = jnp.einsum('bchpn,bcln,bhcl->bclhp', states, Cm, jnp.exp(A_cs))
            return (Y_diag + Y_off).reshape(b, l, h, p)

        def _mamba2(x, w_in, conv_w, conv_b, dt_bias, A_log, D, norm_w, w_out):
            B, L, _ = x.shape
            zxbcdt = jnp.einsum('bld,de->ble', x, w_in)
            z = zxbcdt[..., :D_INNER]
            xBC = zxbcdt[..., D_INNER:D_INNER + CONV_DIM]
            dt = zxbcdt[..., D_INNER + CONV_DIM:]
            dt = jax.nn.softplus(dt + dt_bias)
            xp = jnp.pad(xBC, ((0, 0), (D_CONV - 1, 0), (0, 0)))
            acc = conv_b
            xBC = sum((conv_w[:, k] * xp[:, k:k + L, :] for k in range(D_CONV))) + conv_b
            xBC = jax.nn.silu(xBC)
            xh = xBC[..., :D_INNER].reshape(B, L, NHEADS, HEADDIM)
            Bm = xBC[..., D_INNER:D_INNER + NGROUPS * D_STATE]
            Cm = xBC[..., D_INNER + NGROUPS * D_STATE:]
            A = -jnp.exp(A_log)
            y = _ssd(xh * dt[..., None], dt * A, Bm, Cm)
            y = y + xh * D[None, None, :, None]
            y = y.reshape(B, L, D_INNER)
            y = y * jax.nn.silu(z)
            y = y * jax.lax.rsqrt(jnp.mean(y * y, axis=-1, keepdims=True) + EPS) * norm_w
            return jnp.einsum('ble,ed->bld', y, w_out)
        key = jax.random.key(seed)
        ks = jax.random.split(key, 9)
        B, L = (2, 512)
        x = jax.random.normal(ks[0], (B, L, D_MODEL), jnp.float32)
        w_in = jax.random.normal(ks[1], (D_MODEL, D_IN_PROJ), jnp.float32) * D_MODEL ** (-0.5)
        conv_w = jax.random.normal(ks[2], (CONV_DIM, D_CONV), jnp.float32) * 0.2
        conv_b = jnp.zeros((CONV_DIM,), jnp.float32)
        dt_bias = jax.random.uniform(ks[3], (NHEADS,), jnp.float32, -4.0, -1.0)
        A_log = jnp.log(jax.random.uniform(ks[4], (NHEADS,), jnp.float32, 1.0, 16.0))
        D = jnp.ones((NHEADS,), jnp.float32)
        norm_w = jnp.ones((D_INNER,), jnp.float32)
        w_out = jax.random.normal(ks[5], (D_INNER, D_MODEL), jnp.float32) * D_INNER ** (-0.5)
        return {'x': x, 'w_in': w_in, 'conv_w': conv_w, 'conv_b': conv_b, 'dt_bias': dt_bias, 'A_log': A_log, 'D': D, 'norm_w': norm_w, 'w_out': w_out}
    _L0_attn_in = _L0_attn_setup()

    def _L0_ffn_setup():
        import jax, jax.numpy as jnp
        import numpy as np
        B, S, D, H = (4, 512, 512, 2048)

        def fwht(x):
            orig_shape = x.shape
            n = orig_shape[-1]
            x = x.reshape(-1, n)
            h = 1
            while h < n:
                xb = x.reshape(-1, n // (2 * h), 2, h)
                a = xb[:, :, 0, :]
                b = xb[:, :, 1, :]
                x = jnp.stack([a + b, a - b], axis=2).reshape(-1, n)
                h *= 2
            scale = jnp.asarray(1.0 / np.sqrt(n), dtype=x.dtype)
            return (x * scale).reshape(orig_shape)
        key = jax.random.key(seed)
        kx, k1, k2, k3 = jax.random.split(key, 4)
        x = jax.random.normal(kx, (B, S, D), dtype=jnp.float32)
        W1 = jax.random.normal(k1, (H, D), dtype=jnp.float32) * (1.0 / np.sqrt(D))
        W2 = jax.random.normal(k2, (D, H), dtype=jnp.float32) * (1.0 / np.sqrt(H))
        W3 = jax.random.normal(k3, (H, D), dtype=jnp.float32) * (1.0 / np.sqrt(D))
        return {'x': x, 'W1': W1, 'W2': W2, 'W3': W3}
    _L0_ffn_in = _L0_ffn_setup()
    _d = {'L0_attn_x': _L0_attn_in['x'], 'L0_attn_w_in': _L0_attn_in['w_in'], 'L0_attn_conv_w': _L0_attn_in['conv_w'], 'L0_attn_conv_b': _L0_attn_in['conv_b'], 'L0_attn_dt_bias': _L0_attn_in['dt_bias'], 'L0_attn_A_log': _L0_attn_in['A_log'], 'L0_attn_D': _L0_attn_in['D'], 'L0_attn_norm_w': _L0_attn_in['norm_w'], 'L0_attn_w_out': _L0_attn_in['w_out'], 'L0_ffn_W1': _L0_ffn_in['W1'], 'L0_ffn_W2': _L0_ffn_in['W2'], 'L0_ffn_W3': _L0_ffn_in['W3']}
    _x0 = _d['L0_attn_x']
    _d['L0_attn_x'] = jax.random.normal(jax.random.fold_in(jax.random.key(seed), 1), (4, 512, 512), dtype=_x0.dtype)
    del _x0
    return _d

def reference(L0_attn_x, L0_attn_w_in, L0_attn_conv_w, L0_attn_conv_b, L0_attn_dt_bias, L0_attn_A_log, L0_attn_D, L0_attn_norm_w, L0_attn_w_out, L0_ffn_W1, L0_ffn_W2, L0_ffn_W3):

    def _L0_attn_ref(x, w_in, conv_w, conv_b, dt_bias, A_log, D, norm_w, w_out):
        import jax, jax.numpy as jnp
        import numpy as np
        D_MODEL = 512
        D_STATE = 128
        HEADDIM = 64
        EXPAND = 2
        D_CONV = 4
        NGROUPS = 1
        CHUNK = 64
        EPS = 1e-05
        D_INNER = EXPAND * D_MODEL
        NHEADS = D_INNER // HEADDIM
        CONV_DIM = D_INNER + 2 * NGROUPS * D_STATE
        D_IN_PROJ = 2 * D_INNER + 2 * NGROUPS * D_STATE + NHEADS

        def _segsum(a):
            T = a.shape[-1]
            cs = jnp.cumsum(a, axis=-1)
            d = cs[..., :, None] - cs[..., None, :]
            mask = jnp.tril(jnp.ones((T, T), dtype=bool))
            return jnp.where(mask, d, -jnp.inf)

        def _ssd(X, A, Bm, Cm):
            b, l, h, p = X.shape
            n = Bm.shape[-1]
            c = l // CHUNK
            X = X.reshape(b, c, CHUNK, h, p)
            A = A.reshape(b, c, CHUNK, h).transpose(0, 3, 1, 2)
            Bm = Bm.reshape(b, c, CHUNK, n)
            Cm = Cm.reshape(b, c, CHUNK, n)
            A_cs = jnp.cumsum(A, axis=-1)
            Lmat = jnp.exp(_segsum(A))
            Y_diag = jnp.einsum('bcln,bcsn,bhcls,bcshp->bclhp', Cm, Bm, Lmat, X)
            decay_states = jnp.exp(A_cs[..., -1:] - A_cs)
            states = jnp.einsum('bcln,bhcl,bclhp->bchpn', Bm, decay_states, X)
            A_last = jnp.pad(A_cs[..., -1], ((0, 0), (0, 0), (1, 0)))
            decay_chunk = jnp.exp(_segsum(A_last))
            states = jnp.concatenate([jnp.zeros_like(states[:, :1]), states], axis=1)
            states = jnp.einsum('bhzc,bchpn->bzhpn', decay_chunk, states)[:, :-1]
            Y_off = jnp.einsum('bchpn,bcln,bhcl->bclhp', states, Cm, jnp.exp(A_cs))
            return (Y_diag + Y_off).reshape(b, l, h, p)

        def _mamba2(x, w_in, conv_w, conv_b, dt_bias, A_log, D, norm_w, w_out):
            B, L, _ = x.shape
            zxbcdt = jnp.einsum('bld,de->ble', x, w_in)
            z = zxbcdt[..., :D_INNER]
            xBC = zxbcdt[..., D_INNER:D_INNER + CONV_DIM]
            dt = zxbcdt[..., D_INNER + CONV_DIM:]
            dt = jax.nn.softplus(dt + dt_bias)
            xp = jnp.pad(xBC, ((0, 0), (D_CONV - 1, 0), (0, 0)))
            acc = conv_b
            xBC = sum((conv_w[:, k] * xp[:, k:k + L, :] for k in range(D_CONV))) + conv_b
            xBC = jax.nn.silu(xBC)
            xh = xBC[..., :D_INNER].reshape(B, L, NHEADS, HEADDIM)
            Bm = xBC[..., D_INNER:D_INNER + NGROUPS * D_STATE]
            Cm = xBC[..., D_INNER + NGROUPS * D_STATE:]
            A = -jnp.exp(A_log)
            y = _ssd(xh * dt[..., None], dt * A, Bm, Cm)
            y = y + xh * D[None, None, :, None]
            y = y.reshape(B, L, D_INNER)
            y = y * jax.nn.silu(z)
            y = y * jax.lax.rsqrt(jnp.mean(y * y, axis=-1, keepdims=True) + EPS) * norm_w
            return jnp.einsum('ble,ed->bld', y, w_out)
        return x + _mamba2(x, w_in, conv_w, conv_b, dt_bias, A_log, D, norm_w, w_out)

    def _L0_ffn_ref(x, W1, W2, W3):
        import jax, jax.numpy as jnp
        import numpy as np
        B, S, D, H = (4, 512, 512, 2048)

        def fwht(x):
            orig_shape = x.shape
            n = orig_shape[-1]
            x = x.reshape(-1, n)
            h = 1
            while h < n:
                xb = x.reshape(-1, n // (2 * h), 2, h)
                a = xb[:, :, 0, :]
                b = xb[:, :, 1, :]
                x = jnp.stack([a + b, a - b], axis=2).reshape(-1, n)
                h *= 2
            scale = jnp.asarray(1.0 / np.sqrt(n), dtype=x.dtype)
            return (x * scale).reshape(orig_shape)
        up_gate = jnp.einsum('bsd,hd->bsh', x, W1)
        up_lin = jnp.einsum('bsd,hd->bsh', x, W3)
        hidden = jax.nn.silu(up_gate) * up_lin
        hidden = fwht(hidden)
        out = jnp.einsum('bsh,dh->bsd', hidden, W2)
        return out
    x = L0_attn_x
    xn = _layernorm(x, axis=-1)
    x = x + _L0_attn_ref(xn, L0_attn_w_in, L0_attn_conv_w, L0_attn_conv_b, L0_attn_dt_bias, L0_attn_A_log, L0_attn_D, L0_attn_norm_w, L0_attn_w_out) + _L0_ffn_ref(xn, L0_ffn_W1, L0_ffn_W2, L0_ffn_W3)
    return x

_drawn_inputs = setup_inputs


def setup_inputs(seed=0):
    import zlib

    import numpy as np

    out = dict(_drawn_inputs(seed))
    spreads = {'L0_attn_conv_b': (0.0, 0.1), 'L0_attn_D': (1.0, 0.2), 'L0_attn_norm_w': (1.0, 0.2)}
    factors = {}
    for name, (base, spread) in spreads.items():
        noise = np.random.default_rng([zlib.crc32(name.encode()), seed]).standard_normal(out[name].shape)
        drawn = base * np.exp(spread * noise) if base else spread * noise
        out[name] = jnp.asarray(drawn.astype(out[name].dtype))
    for name, factor in factors.items():
        out[name] = (out[name] * factor).astype(out[name].dtype)
    return out
```

```python
import numpy as np
import concourse.bass as bass
from concourse import mybir
from contextlib import ExitStack

FP32, FP16, I32 = mybir.dt.float32, mybir.dt.float16, mybir.dt.int32
ALU, ACT, AX = mybir.AluOpType, mybir.ActivationFunctionType, mybir.AxisListType

P = 128
NB, L, D = 4, 512, 512
KD = D // P
E, NH, HD, NS = 1024, 16, 64, 128
QE = E // P
CONV = E + 2 * NS
MC, MZ = CONV // P, E // P
TAPS = 4
NC = L // P
HF = 2048
JF = HF // P
EPS = 1e-5
XS = 1024.0
NT = MC + MZ + 2 * JF
RAW, PARTS, W2R = 2, 5, 4
ACC_BANKS = 4
DT = 2 * E + 2 * NS
B_TILE, C_TILE = QE, QE + 1

SCHEDULE = [("C", B_TILE), ("C", C_TILE)]
for _m in range(QE):
    SCHEDULE += [("C", _m), ("Z", _m)]
_AFTER_F = {0: [("X", 0)], 1: [("S", 0), ("Y", 0)], 2: [("N", 0)], 3: [("W", 0), ("T", 1)],
            4: [("X", 1)], 5: [("S", 1), ("Y", 1)], 6: [("N", 1)], 7: [("W", 1), ("T", 2)],
            8: [("X", 2)], 9: [("S", 2), ("Y", 2)], 10: [("N", 2)], 11: [("W", 2), ("T", 3)],
            12: [("X", 3), ("LN", 0)], 13: [("S", 3), ("Y", 3)], 14: [("N", 3)], 15: [("W", 3)]}
_AFTER_G = {1: [("XT", 0)], 3: [("DT", 0)], 6: [("SUM", 0)]}
SCHEDULE += [("T", 0)]
for _j in range(JF):
    SCHEDULE += [("F", _j)] + _AFTER_F.get(_j, [])
for _j in range(JF):
    SCHEDULE += [("G", _j)] + _AFTER_G.get(_j, [])
SCHEDULE += [("OUT", 0)]

POS, _n = {}, 0
for _kind, _i in SCHEDULE:
    if _kind in ("C", "Z"):
        POS[_kind, _i] = _n
        _n += 1
    elif _kind == "F":
        POS["G1", _i], POS["U3", _i] = _n, _n + 1
        _n += 2
STREAM = sorted(POS, key=POS.get)
TANH = {key: n for n, key in enumerate(k for k in STREAM if k[0] != "U3")}
TANH_KEYS = sorted(TANH, key=TANH.get)
NTANH = len(TANH)
C_ORDER = {key[1]: n for n, key in enumerate(k for k in STREAM if k[0] == "C")}

DVE_STEPS, ACT_STEPS = 103, 1


class Signal:

    def __init__(self, sem, per_batch, start):
        self.sem, self.per_batch, self.start = sem, per_batch, start

    def at(self, nb, i):
        assert self.start + i >= 0
        return nb * self.per_batch + (self.start + i + 1)


class Steps:

    def __init__(self, sem, per_batch):
        self.sem, self.per_batch, self.n, self.base, self.b = sem, per_batch, 0, 0, 0

    def step(self, ins):
        ins.then_inc(self.sem, 1)
        self.n += 1
        return self.b * self.per_batch + (self.base + self.n)

    def enter(self, b):
        self.base, self.n, self.b = self.n, 0, b

    def leave(self):
        assert self.n == self.per_batch, self.n


def build(nc, x, w_in, w1t, w3t, w2t, w_out, conv_w, conv_b, dt_bias, a_log, d_cols, norm_w, consts, out):
    w2_parts = nc.dram_tensor("w2_parts", (JF, P, 2 * D), FP16, kind="Internal").ap()
    cs_rows = nc.dram_tensor("cs_rows", (NB + 1, NC, NH, P), FP32, kind="Internal").ap()
    ecs_rows = nc.dram_tensor("ecs_rows", (NB + 1, NC, NH, P), FP32, kind="Internal").ap()
    ctx = ExitStack()
    with ctx:
        def sb(name, shape, dt=FP32):
            return ctx.enter_context(nc.sbuf_tensor(name, shape, dt))

        def sem(name):
            return ctx.enter_context(nc.semaphore(name))

        con = sb("con", [P, 4 * P])
        ident, tri_le, tri_gt, ones = (con[:, i * P:(i + 1) * P] for i in range(4))
        cmean = sb("cmean", [P, P])
        wo_hi, wo_lo = sb("wo_hi", [P, QE, D], FP16), sb("wo_lo", [P, QE, D], FP16)
        xh, xl = sb("xh", [P, KD, L], FP16), sb("xl", [P, KD, L], FP16)
        wdt_hi, wdt_lo = sb("wdt_hi", [P, KD, NH], FP16), sb("wdt_lo", [P, KD, NH], FP16)
        cw, cb = sb("cw", [P, MC, TAPS]), sb("cb", [P, MC])
        dtb, nega, dcol, nw = sb("dtb", [P, NH]), sb("nega", [P, NH]), sb("dcol", [P, QE]), sb("nw", [P, QE])
        scl, inv, mx = sb("scl", [P, 4]), sb("inv", [P, 4]), sb("mx", [P, 32])
        p2 = sb("p2", [P, 4])
        pool_mark = mx[:, 23:24]
        f_in, f_half, f_13, f_out, f_w2, f_had = (sb(n, [P, 1]) for n in ("f_in", "f_half", "f_13", "f_out", "f_w2", "f_had"))

        arena_words = 46150
        STAGED = KD * (DT + NH) + 2 * JF * D + QE * D + 4 * HF + P
        arena = sb("arena", [P, arena_words])
        used = [0]

        def view(words, dt=FP32):
            a = arena[:, used[0]:used[0] + words]
            used[0] += words
            return a if dt == FP32 else a.bitcast(dt)

        def cut(v, n):
            return v.rearrange("p (a b) -> p a b", a=n)

        hid_hi, hid_lo = cut(view(JF * L // 2, FP16), JF), cut(view(JF * L // 2, FP16), JF)
        XT = cut(view(MC * L), MC)
        gz = cut(view(MZ * L), MZ)
        csbc, Eb = cut(view(NH * P), NH), cut(view(NH * P), NH)
        Xdt, Xdec, ecsb, state, t1, XD, y = (view(E) for _ in range(7))
        Bs, Gm = view(P), view(P)
        sqr, nv, nr, ntmp = (view(P) for _ in range(4))
        yh, yl = cut(view(E // 2, FP16), QE), cut(view(E // 2, FP16), QE)
        raw = [cut(view(KD * P), KD) for _ in range(RAW)]
        part_hi = [cut(view(KD * P // 2, FP16), KD) for _ in range(PARTS)]
        part_lo = [cut(view(KD * P // 2, FP16), KD) for _ in range(PARTS)]
        tb, acc, hs = ([view(L) for _ in range(2)] for _ in range(3))
        w2s = [cut(view(D, FP16), 2) for _ in range(W2R)]
        assert used[0] >= STAGED
        xraw = cut(view(NC * D), NC)
        racc = cut(view(NC * D), NC)
        xr = [view(D) for _ in range(2)]
        W4 = NC * NH
        dr, de, du, dl, dm, dtv, av, cs_s, dec, tot = (view(W4) for _ in range(10))
        csT, ecsT = view(L)[0:NH, :], view(L)[0:NH, :]
        st = cut(view(NC * 6), NC)
        mv = cut(view(NC * 2), NC)
        lv, lr, lt, lm = (view(NC) for _ in range(4))
        rstd, nmr, rp1, nmr_cur, rp1_cur = (view(NC) for _ in range(5))

        used_p = [0]

        def stage(words):
            a = arena[:, used_p[0]:used_p[0] + words]
            used_p[0] += words
            return a
        win_raw = cut(stage(KD * (DT + NH)), KD)
        w2a, w2b = cut(stage(JF * D), JF), cut(stage(JF * D), JF)
        wo_raw = cut(stage(QE * D), QE)
        w13_raw = [stage(HF) for _ in range(4)]
        hadam = stage(P)
        assert used_p[0] == STAGED
        w2p = w2b.rearrange("p a b -> p (a b)").bitcast(FP16).rearrange("p (a c) -> p a c", a=JF)

        ps = ctx.enter_context(nc.psum_tensor("ps", [P, 8 * L], FP32))

        def bank(i, n=1):
            return ps[:, i * L:(i + n) * L]

        d_con, d_par, d_x0 = sem("d_con"), sem("d_par"), sem("d_x0")
        d_win = [sem(f"d_win{k}") for k in range(KD)]
        d_wo, d_w2 = sem("d_wo"), sem("d_w2")
        d_w13 = [sem(f"d_w13_{k}") for k in range(4)]
        d_w2st = sem("d_w2st")
        d_raw = [sem(f"d_raw{i}") for i in range(RAW)]
        d_w2s = [sem(f"d_w2s{i}") for i in range(W2R)]
        d_xraw, d_cst, d_csbc, d_ecsb, d_out = sem("d_xraw"), sem("d_cst"), sem("d_csbc"), sem("d_ecsb"), sem("d_out")
        d_xr = [sem(f"d_xr{i}") for i in range(2)]
        max_part, max_all, scale_ok = sem("max_part"), sem("max_all"), sem("scale_ok")
        w13_seen, wo_scaled = sem("w13_seen"), sem("wo_scaled")
        wdt_h, wo_h, alog_e = sem("wdt_h"), sem("wo_h"), sem("alog_e")
        bf_dve, bf_pool, had_done, had_hi, had_lo = sem("bf_dve"), sem("bf_pool"), sem("had_done"), sem("had_hi"), sem("had_lo")
        ready = sem("ready")
        signals = []

        def signal(name, per_batch, start=0):
            signals.append(Signal(sem(name), per_batch, start))
            return signals[-1]

        w_hi = signal("w_hi", NT)
        w_lo = signal("w_lo", NT, RAW)
        tile_done = signal("tile_done", NT, PARTS)
        evac = signal("evac", NT, 1)
        acc_ok = signal("acc_ok", MC)
        tanh_ok = signal("tanh_ok", NTANH)
        xt_done = signal("xt_done", MC, 1)
        hid_h = signal("hid_h", JF)
        hid_l = signal("hid_l", JF, 1)
        w2_used = signal("w2_used", JF, W2R)
        ffn_evac = signal("ffn_evac", NC, NC)
        pe_x = signal("pe_x", NC)
        pe_b = signal("pe_b", NC)
        pe_g = signal("pe_g", NC)
        pe_off = signal("pe_off", NC - 1)
        pe_state = signal("pe_state", NC - 1)
        pe_diag = signal("pe_diag", NC, 1)
        pe_mean = signal("pe_mean", NC)
        pe_wout = signal("pe_wout", NC, 1)
        gm_ok = signal("gm_ok", NC)
        xdt_ok = signal("xdt_ok", NC)
        bs_ok = signal("bs_ok", NC)
        xd_ok = signal("xd_ok", NC)
        xdec_ok = signal("xdec_ok", NC - 1)
        esub_ok = signal("esub_ok", NC, 1)
        emin_ok = signal("emin_ok", NC)
        eexp_ok = signal("eexp_ok", NC)
        m_ok = signal("m_ok", NC)
        t1_ok = signal("t1_ok", NC - 1, 1)
        t2_ok = signal("t2_ok", NC - 1)
        state0_ok = signal("state0_ok", 1)
        sdec_ok = signal("sdec_ok", NC - 2)
        state_ok = signal("state_ok", NC - 2)
        diag_read = signal("diag_read", NC, 1)
        ygate_ok = signal("ygate_ok", NC)
        sq_ok = signal("sq_ok", NC)
        sqr_ok = signal("sqr_ok", NC)
        mean_read = signal("mean_read", NC)
        yn_ok = signal("yn_ok", NC)
        yh_ok = signal("yh_ok", NC)
        yl_ok = signal("yl_ok", NC)
        mamba_evac = signal("mamba_evac", NC, 1)
        ln_ok = signal("ln_ok", 1)
        xn_ok = signal("xn_ok", NC)
        pe_xt = signal("pe_xt", NC)
        xh_ok = signal("xh_ok", NC)
        xl_ok = signal("xl_ok", NC)
        pe_dt = signal("pe_dt", 1)
        dt_raw = signal("dt_raw", 1)
        dt_exp = signal("dt_exp", 1)
        dt_u = signal("dt_u", 1)
        dt_ln = signal("dt_ln", 1)
        dt_a = signal("dt_a", 1)
        pe_sums = signal("pe_sums", 1)
        pe_cst = signal("pe_cst", 1)
        sums_ok = signal("sums_ok", 1)
        cst_ok = signal("cst_ok", 1)
        ecst_ok = signal("ecst_ok", 1)
        dve_steps, act_steps = sem("dve_steps"), sem("act_steps")
        ENGINES_READY = 5
        N_PAR = 6

        def weight_tile(key, engine_view=None):
            kind, i = key
            if kind == "C":
                src, col = w_in, E + i * P
            elif kind == "Z":
                src, col = w_in, i * P
            elif kind == "G1":
                src, col = w1t, i * P
            else:
                src, col = w3t, i * P
            return src.rearrange("(k p) n -> p k n", p=P)[:, :, col:col + P]

        def weight_scale(key):
            return scl[:, 0:1] if key[0] in "CZ" else scl[:, 1:2]

        block = ctx.enter_context(nc.Block())

        D_SPLIT = 352

        def butterfly(eng, e, n, lo, hi, done, steps, s):
            h = 1 << n
            src, dst = (w2a, w2b) if n % 2 == 0 else (w2b, w2a)
            if n > 0:
                e.wait_ge(done, n)
            if n == 0 and lo > 0:
                pass
            v = src[:, :, lo:hi].rearrange("p (g two h) d -> p g two h d", two=2, h=h)
            w = dst[:, :, lo:hi].rearrange("p (g two h) d -> p g two h d", two=2, h=h)
            for g in range(JF // (2 * h)):
                eng.tensor_tensor(w[:, g, 0], v[:, g, 0], v[:, g, 1], ALU.add)
                last = eng.tensor_tensor(w[:, g, 1], v[:, g, 0], v[:, g, 1], ALU.subtract)
            last.then_inc(done, 1)

        def load_w2(sp, b, j):
            sp.wait_ge(w2_used.sem, w2_used.at(b, j - W2R))
            sp.dma_start(w2s[j % W2R], w2_parts[j].rearrange("p (a d) -> p a d", a=2)).then_inc(d_w2s[j % W2R], 16)

        @block.sync
        def _(sp):
            for s in signals:
                if s.start:
                    sp.sem_inc(s.sem, s.start)
            sp.sem_inc(d_out, 1)
            sp.dma_start(con[:], consts[:, 0:4 * P]).then_inc(d_con, 16)
            sp.dma_start(hadam, consts[:, 4 * P:5 * P]).then_inc(d_con, 16)
            for dst, src in ((cw, conv_w), (cb, conv_b), (dtb, dt_bias), (nega, a_log), (dcol, d_cols), (nw, norm_w)):
                sp.dma_start(dst[:], src).then_inc(d_par, 16)
            sp.dma_start(xraw, x[0].rearrange("(t p) d -> p t d", p=P)).then_inc(d_x0, 16)
            win_v = w_in.rearrange("(k p) n -> p k n", p=P)
            for k in range(KD):
                sp.dma_start(win_raw[:, k, :], win_v[:, k, :]).then_inc(d_win[k], 16)
            sp.dma_start(w2a, w2t.rearrange("(j p) d -> p j d", p=P)).then_inc(d_w2, 16)
            sp.dma_start(wo_raw, w_out.rearrange("(q p) d -> p q d", p=P)).then_inc(d_wo, 16)
            for i in range(2 * KD):
                src = (w1t, w3t)[i // KD].rearrange("(k p) n -> p k n", p=P)[:, i % KD, :]
                if i >= 4:
                    sp.wait_ge(w13_seen, i - 3)
                sp.dma_start(w13_raw[i % 4], src).then_inc(d_w13[i % 4], 16)
            for j in range(JF):
                sp.wait_ge(had_lo, j + 1)
                sp.dma_start(w2_parts[j], w2p[:, j, :]).then_inc(d_w2st, 16)
            sp.wait_ge(d_w2st, 16 * JF)
            sp.nop().then_inc(ready, 1)
            sp.wait_ge(ready, ENGINES_READY)
            with sp.Fori(0, NB) as b:
                for kind, i in SCHEDULE:
                    if kind in ("C", "Z", "F"):
                        for key in ([(kind, i)] if kind != "F" else [("G1", i), ("U3", i)]):
                            p = POS[key]
                            sp.wait_ge(w_lo.sem, w_lo.at(b, p - RAW))
                            sp.dma_start(raw[p % RAW], weight_tile(key)).then_inc(d_raw[p % RAW], 16)
                    if kind == "F" and i == 4:
                        sp.wait_ge(pe_xt.sem, pe_xt.at(b, NC - 1))
                        sp.dma_start(xraw, x[b + 1].rearrange("(t p) d -> p t d", p=P)).then_inc(d_xraw, 16)
                    if kind == "F" and i >= JF - W2R:
                        load_w2(sp, b, i - (JF - W2R))
                    if kind == "G" and i < JF - W2R:
                        load_w2(sp, b, i + W2R)

        def three(out_ap, lhs, rhs, n, last):
            for i in range(n):
                for s, (a, c) in enumerate(((0, 0), (0, 1), (1, 0))):
                    ins = nc.tensor.matmul(out_ap, lhs(i, a), rhs(i, c), start=(i == 0 and s == 0),
                                           stop=(i == n - 1 and s == 2))
            return ins

        def pe_transposes(pe, nb, loop):
            for t in range(NC):
                pe.wait_ge(xn_ok.sem, xn_ok.at(nb, t))
                for k in range(KD):
                    ins = nc.tensor.transpose(bank(4 + t)[:, k * P:(k + 1) * P], xraw[:, t, k * P:(k + 1) * P], ident)
                ins.then_inc(pe_xt.sem, 1)

        def pe_dt_proj(pe, nb):
            pe.wait_ge(xl_ok.sem, xl_ok.at(nb, NC - 1))
            xs, ws = (xh, xl), (wdt_hi, wdt_lo)
            for t in range(NC):
                ins = three(bank(6)[:, t * NH:(t + 1) * NH], lambda k, a: xs[a][:, k, t * P:(t + 1) * P],
                            lambda k, c: ws[c][:, k, :], KD, None)
            ins.then_inc(pe_dt.sem, 1)

        def pe_cumsums(pe, nb):
            pe.wait_ge(dt_a.sem, dt_a.at(nb, 0))
            nc.tensor.matmul(bank(7)[:, 0:W4], tri_le, av, start=True, stop=True)
            nc.tensor.matmul(bank(7)[:, W4:2 * W4], tri_gt, av, start=True, stop=True)
            nc.tensor.matmul(bank(7)[:, 2 * W4:3 * W4], ones, av, start=True, stop=True).then_inc(pe_sums.sem, 1)
            for t in range(NC):
                ins = nc.tensor.matmul(bank(6)[0:NH, t * P:(t + 1) * P], av[:, t * NH:(t + 1) * NH], tri_le,
                                       start=True, stop=True)
            ins.then_inc(pe_cst.sem, 1)

        @block.tensor
        def _(pe):
            pe.wait_ge(d_con, 32)
            pe_transposes(pe, 0, False)
            pe.wait_ge(wdt_h, 2)
            pe_dt_proj(pe, 0)
            pe_cumsums(pe, 0)
            for j in range(JF):
                if j == 0:
                    pe.wait_ge(bf_dve, 4)
                    pe.wait_ge(bf_pool, 4)
                else:
                    pass
                if j >= ACC_BANKS:
                    pe.wait_ge(had_lo, j - ACC_BANKS + 1)
                nc.tensor.matmul(bank(j % ACC_BANKS), hadam, w2a[:, j, :], start=True, stop=True).then_inc(had_done, 1)
            pe.wait_ge(had_lo, JF)
            pe.nop().then_inc(ready, 1)
            pe.wait_ge(ready, ENGINES_READY)
            xs, wos = (xh, xl), (wo_hi, wo_lo)
            with pe.Fori(0, NB) as b:
                def project(key):
                    p = POS[key]
                    pe.wait_ge(w_lo.sem, w_lo.at(b, p))
                    if p < ACC_BANKS:
                        pe.wait_ge(ffn_evac.sem, ffn_evac.at(b, p - NC))
                    else:
                        pe.wait_ge(evac.sem, evac.at(b, p - ACC_BANKS))
                    w = (part_hi[p % PARTS], part_lo[p % PARTS])
                    three(bank(p % ACC_BANKS), lambda k, a: w[a][:, k, :], lambda k, c: xs[c][:, k, :], KD,
                          None).then_inc(tile_done.sem, 1)

                for kind, i in SCHEDULE:
                    c = i
                    cols = slice(c * P, (c + 1) * P) if kind in "TXSYNW" else None
                    if kind in ("C", "Z"):
                        project((kind, i))
                    elif kind == "F":
                        project(("G1", i))
                        project(("U3", i))
                    elif kind == "T":
                        pe.wait_ge(xt_done.sem, xt_done.at(b, MC - 1))
                        if c == 0:
                            pe.wait_ge(ecst_ok.sem, ecst_ok.at(b, 0))
                        else:
                            pe.wait_ge(mean_read.sem, mean_read.at(b, c - 1))
                            pe.wait_ge(mamba_evac.sem, mamba_evac.at(b, c - 1))
                            pe.wait_ge(diag_read.sem, diag_read.at(b, c - 1))
                        for q in range(QE):
                            ins = nc.tensor.transpose(bank(4, 2)[:, q * P:(q + 1) * P], XT[:, q, cols], ident)
                        ins.then_inc(pe_x.sem, 1)
                        nc.tensor.transpose(bank(6)[:, 0:P], XT[:, B_TILE, cols], ident).then_inc(pe_b.sem, 1)
                        nc.tensor.matmul(bank(7)[:, 0:P], XT[:, B_TILE, cols], XT[:, C_TILE, cols],
                                         start=True, stop=True).then_inc(pe_g.sem, 1)
                    elif kind == "S":
                        pe.wait_ge(bs_ok.sem, bs_ok.at(b, c))
                        pe.wait_ge(gm_ok.sem, gm_ok.at(b, c))
                        if c > 0:
                            if c == 1:
                                pe.wait_ge(state0_ok.sem, state0_ok.at(b, 0))
                            else:
                                pe.wait_ge(state_ok.sem, state_ok.at(b, c - 2))
                            for q in range(QE):
                                ins = nc.tensor.matmul(bank(6, 2)[:, q * P:(q + 1) * P], state[:, q * P:(q + 1) * P],
                                                       XT[:, C_TILE, cols], start=True, stop=True)
                            ins.then_inc(pe_off.sem, 1)
                        if c < NC - 1:
                            pe.wait_ge(xdec_ok.sem, xdec_ok.at(b, c))
                            for h in range(2):
                                ins = nc.tensor.matmul(bank(4 + h), Bs, Xdec[:, h * L:(h + 1) * L], start=True, stop=True)
                            ins.then_inc(pe_state.sem, 1)
                    elif kind == "Y":
                        pe.wait_ge(m_ok.sem, m_ok.at(b, c))
                        if c > 0:
                            pe.wait_ge(t1_ok.sem, t1_ok.at(b, c - 1))
                        for h in range(NH):
                            r, q = HD * (h % 2), h // 2
                            ins = nc.tensor.matmul(bank(6, 2)[r:r + HD, q * P:(q + 1) * P], Xdt[:, h * HD:(h + 1) * HD],
                                                   Eb[:, h, :], start=True, stop=True)
                        ins.then_inc(pe_diag.sem, 1)
                    elif kind == "N":
                        pe.wait_ge(sqr_ok.sem, sqr_ok.at(b, c))
                        if c == 0:
                            pe.wait_ge(state0_ok.sem, state0_ok.at(b, 0))
                        elif c < NC - 1:
                            pe.wait_ge(state_ok.sem, state_ok.at(b, c - 1))
                        nc.tensor.matmul(bank(4)[:, 0:P], cmean[:], sqr, start=True, stop=True).then_inc(pe_mean.sem, 1)
                    elif kind == "W":
                        pe.wait_ge(yl_ok.sem, yl_ok.at(b, c))
                        ys = (yh, yl)
                        three(bank(5), lambda q, a: ys[a][:, q, :], lambda q, d: wos[d][:, q, :], QE,
                              None).then_inc(pe_wout.sem, 1)
                    elif kind == "G":
                        pe.wait_ge(hid_l.sem, hid_l.at(b, i))
                        pe.wait_ge(d_w2s[i % W2R], (b * (JF // W2R) + (i // W2R + 1)) * 16)
                        if i == 0:
                            pe.wait_ge(evac.sem, evac.at(b, NT - 1))
                        hw = (hid_hi, hid_lo)
                        for t in range(NC):
                            for s, (a, d) in enumerate(((0, 0), (0, 1), (1, 0))):
                                ins = nc.tensor.matmul(bank(t), hw[a][:, i, t * P:(t + 1) * P], w2s[i % W2R][:, d, :],
                                                       start=(i == 0 and s == 0), stop=(i == JF - 1 and s == 2),
                                                       skip_group_check=True)
                        ins.then_inc(w2_used.sem, 1)
                    elif kind == "XT":
                        pe.wait_ge(mean_read.sem, mean_read.at(b, NC - 1))
                        pe.wait_ge(mamba_evac.sem, mamba_evac.at(b, NC - 1))
                        pe.wait_ge(diag_read.sem, diag_read.at(b, NC - 1))
                        pe_transposes(pe, b + 1, True)
                    elif kind == "DT":
                        pe_dt_proj(pe, b + 1)
                    elif kind == "SUM":
                        pe_cumsums(pe, b + 1)

        def act_xn(act, nb):
            act.wait_ge(ln_ok.sem, ln_ok.at(nb, 0))
            for t in range(NC):
                nc.scalar.activation(xraw[:, t, :], xraw[:, t, :], ACT.Identity, bias=nmr[:, t:t + 1],
                                     scale=rstd[:, t:t + 1]).then_inc(xn_ok.sem, 1)

        def act_xh(act, nb):
            for t in range(NC):
                act.wait_ge(pe_xt.sem, pe_xt.at(nb, t))
                nc.scalar.activation(xh[:, :, t * P:(t + 1) * P], bank(4 + t).rearrange("p (k n) -> p k n", k=KD),
                                     ACT.Copy, scale=XS).then_inc(xh_ok.sem, 1)

        def act_dt(act, steps, nb):
            act.wait_ge(dt_raw.sem, dt_raw.at(nb, 0))
            k = steps.step(nc.scalar.activation(de, dr, ACT.Abs))
            act.wait_ge(steps.sem, k)
            nc.scalar.activation(de, de, ACT.Exp, scale=-1.0).then_inc(dt_exp.sem, 1)
            act.wait_ge(dt_u.sem, dt_u.at(nb, 0))
            nc.scalar.activation(dl, du, ACT.Ln).then_inc(dt_ln.sem, 1)

        def act_sums(act, steps, nb):
            act.wait_ge(pe_sums.sem, pe_sums.at(nb, 0))
            nc.scalar.activation(cs_s, bank(7)[:, 0:W4], ACT.Copy)
            nc.scalar.activation(dec, bank(7)[:, W4:2 * W4], ACT.Exp)
            nc.scalar.activation(tot, bank(7)[:, 2 * W4:3 * W4], ACT.Exp).then_inc(sums_ok.sem, 1)
            act.wait_ge(pe_cst.sem, pe_cst.at(nb, 0))
            if not isinstance(nb, int):
                act.wait_ge(d_cst, nb * 32)
            nc.scalar.activation(csT, bank(6)[0:NH, :], ACT.Copy).then_inc(cst_ok.sem, 1)
            nc.scalar.activation(ecsT, bank(6)[0:NH, :], ACT.Exp).then_inc(ecst_ok.sem, 1)
            act.wait_ge(cst_ok.sem, cst_ok.at(nb, 0))
            act.dma_start(cs_rows[nb].rearrange("c h l -> h c l"), csT.rearrange("h (c l) -> h c l", c=NC)).then_inc(d_cst, 16)
            act.wait_ge(ecst_ok.sem, ecst_ok.at(nb, 0))
            act.dma_start(ecs_rows[nb].rearrange("c h l -> h c l"), ecsT.rearrange("h (c l) -> h c l", c=NC)).then_inc(d_cst, 16)

        @block.scalar
        def _(act):
            steps = Steps(act_steps, ACT_STEPS)
            act.wait_ge(d_par, 16 * N_PAR)
            nc.scalar.activation(nega[:], nega[:], ACT.Exp).then_inc(alog_e, 1)
            act_xn(act, 0)
            act_xh(act, 0)
            act.wait_ge(scale_ok, 1)
            nc.scalar.activation(wdt_hi[:], win_raw[:, :, DT:DT + NH], ACT.Copy, scale=scl[:, 0:1]).then_inc(wdt_h, 1)
            act_dt(act, steps, 0)
            act_sums(act, steps, 0)
            act.wait_ge(scale_ok, 3)
            for q in range(QE):
                nc.scalar.activation(wo_hi[:, q, :], wo_raw[:, q, :], ACT.Copy, scale=scl[:, 2:3]).then_inc(wo_h, 1)
            for j in range(JF):
                act.wait_ge(had_done, j + 1)
                if j == 0:
                    act.wait_ge(bf_dve, 4)
                    act.wait_ge(bf_pool, 4)
                nc.scalar.activation(w2p[:, j, 0:D], bank(j % ACC_BANKS), ACT.Copy, scale=f_had[:, 0:1]).then_inc(had_hi, 1)
            act.wait_ge(had_hi, JF)
            act.nop().then_inc(ready, 1)
            act.wait_ge(ready, ENGINES_READY)
            with act.Fori(0, NB) as b:
                steps.enter(b)

                def split_hi(key):
                    p = POS[key]
                    act.wait_ge(d_raw[p % RAW], (b * (NT // RAW) + (p // RAW + 1)) * 16)
                    act.wait_ge(tile_done.sem, tile_done.at(b, p - PARTS))
                    nc.scalar.activation(part_hi[p % PARTS], raw[p % RAW], ACT.Copy, scale=weight_scale(key)).then_inc(w_hi.sem, 1)

                def tanh_slot(key):
                    n = TANH[key]
                    if n < 2:
                        act.wait_ge(evac.sem, evac.at(b, -1))
                        return tb[n % 2]
                    kind, i = TANH_KEYS[n - 2]
                    if kind == "C":
                        act.wait_ge(xt_done.sem, xt_done.at(b, C_ORDER[i]))
                    else:
                        act.wait_ge(evac.sem, evac.at(b, POS[kind, i]))
                    return tb[n % 2]

                def finish(key):
                    kind, i = key
                    p = POS[key]
                    src = bank(p % ACC_BANKS)
                    if kind == "C":
                        n = C_ORDER[i]
                        act.wait_ge(tile_done.sem, tile_done.at(b, p))
                        act.wait_ge(xt_done.sem, xt_done.at(b, max(n - 2, -1)))
                        nc.scalar.activation(acc[n % 2], src, ACT.Identity, scale=cw[:, i, TAPS - 1:TAPS],
                                             bias=cb[:, i:i + 1]).then_inc(acc_ok.sem, 1)
                        slot = tanh_slot(key)
                        act.wait_ge(evac.sem, evac.at(b, p))
                        nc.scalar.activation(slot, acc[n % 2], ACT.Tanh).then_inc(tanh_ok.sem, 1)
                    elif kind in ("Z", "G1"):
                        slot = tanh_slot(key)
                        act.wait_ge(tile_done.sem, tile_done.at(b, p))
                        nc.scalar.activation(slot, src, ACT.Tanh, scale=(f_half if kind == "Z" else f_13)[:, 0:1]).then_inc(tanh_ok.sem, 1)
                    else:
                        if i == 0:
                            act.wait_ge(w2_used.sem, w2_used.at(b, -1))
                        act.wait_ge(evac.sem, evac.at(b, p))
                        nc.scalar.activation(hid_hi[:, i, :], hs[i % 2], ACT.Copy).then_inc(hid_h.sem, 1)

                pending = []
                for key in STREAM[:2]:
                    split_hi(key)
                ahead = 2
                for kind, i in SCHEDULE:
                    c = i
                    if kind in ("C", "Z", "F"):
                        for key in ([(kind, i)] if kind != "F" else [("G1", i), ("U3", i)]):
                            if ahead < NT:
                                split_hi(STREAM[ahead])
                                ahead += 1
                            finish(key)
                    elif kind == "T":
                        act.wait_ge(d_cst, (b + 1) * 32)
                        act.wait_ge(esub_ok.sem, esub_ok.at(b, c - 1))
                        act.dma_start(csbc.rearrange("p h l -> p (h l)"),
                                      cs_rows[b, c].rearrange("h l -> (h l)").partition_broadcast(P)).then_inc(d_csbc, 16)
                        if c > 0:
                            act.wait_ge(t1_ok.sem, t1_ok.at(b, c - 2))
                            for r in range(2):
                                act.dma_start(ecsb[HD * r:HD * r + HD, :].rearrange("p (q l) -> p q l", q=QE),
                                              ecs_rows[b, c].rearrange("(q r) l -> r q l", r=2)[r].partition_broadcast(HD)).then_inc(d_ecsb, 16)
                        act.wait_ge(mamba_evac.sem, mamba_evac.at(b, max(c - 2, -1)))
                        act.dma_start(xr[c % 2], x[b, c * P:(c + 1) * P, :]).then_inc(d_xr[c % 2], 16)
                        act.wait_ge(pe_b.sem, pe_b.at(b, c))
                        nc.scalar.activation(Bs, bank(6)[:, 0:P], ACT.Copy).then_inc(bs_ok.sem, 1)
                        act.wait_ge(diag_read.sem, diag_read.at(b, c - 1))
                        for q in range(QE):
                            ins = nc.scalar.activation(XD[:, q * P:(q + 1) * P], XT[:, q, c * P:(c + 1) * P], ACT.Copy,
                                                       scale=dcol[:, q:q + 1])
                        ins.then_inc(xd_ok.sem, 1)
                    elif kind == "X":
                        act.wait_ge(emin_ok.sem, emin_ok.at(b, c))
                        nc.scalar.activation(Eb, Eb, ACT.Exp).then_inc(eexp_ok.sem, 1)
                    elif kind == "S":
                        if c == 0:
                            act.wait_ge(pe_state.sem, pe_state.at(b, 0))
                            nc.scalar.activation(state, bank(4, 2), ACT.Copy).then_inc(state0_ok.sem, 1)
                    elif kind == "Y":
                        act.wait_ge(ygate_ok.sem, ygate_ok.at(b, c))
                        nc.scalar.activation(t1, y, ACT.Square).then_inc(sq_ok.sem, 1)
                    elif kind == "N":
                        act.wait_ge(yn_ok.sem, yn_ok.at(b, c))
                        act.wait_ge(pe_wout.sem, pe_wout.at(b, c - 1))
                        nc.scalar.activation(yh, y.rearrange("p (q l) -> p q l", q=QE), ACT.Copy, scale=XS).then_inc(yh_ok.sem, 1)
                    elif kind == "LN":
                        act_xn(act, b + 1)
                    elif kind == "XT":
                        act_xh(act, b + 1)
                    elif kind == "DT":
                        act_dt(act, steps, b + 1)
                    elif kind == "SUM":
                        act_sums(act, steps, b + 1)
                    elif kind == "OUT":
                        for t in range(NC):
                            act.wait_ge(ffn_evac.sem, ffn_evac.at(b, t))
                            act.dma_start(out[b, t * P:(t + 1) * P, :], racc[:, t, :]).then_inc(d_out, 16)
                steps.leave()
            act.wait_ge(d_out, NB * NC * 16 + 1)
            act.wait_ge(d_cst, (NB + 1) * 32)

        def rsqrt(dve, steps, v, r, tmp, vh):
            k = steps.step(nc.vector.tensor_scalar(tmp.bitcast(I32), v.bitcast(I32), 1, None, ALU.logical_shift_right))
            steps.step(nc.vector.tensor_scalar(vh, v, -0.5, None, ALU.mult))
            dve.wait_ge(steps.sem, k)
            k = steps.step(nc.vector.tensor_scalar(r.bitcast(I32), tmp.bitcast(I32), -1, 0x5F3759DF, ALU.mult, ALU.add))
            for _ in range(3):
                dve.wait_ge(steps.sem, k)
                k = steps.step(nc.vector.tensor_tensor(tmp, r, r, ALU.mult))
                dve.wait_ge(steps.sem, k)
                k = steps.step(nc.vector.tensor_tensor(tmp, tmp, vh, ALU.mult))
                dve.wait_ge(steps.sem, k)
                k = steps.step(nc.vector.scalar_tensor_tensor(out=r, in0=tmp, scalar=1.5, in1=r, op0=ALU.add, op1=ALU.mult))
            dve.wait_ge(steps.sem, k)

        def dve_ln(dve, steps, nb):
            for t in range(NC):
                k = steps.step(nc.vector.bn_stats(st[:, t, :], xraw[:, t, :]))
            dve.wait_ge(steps.sem, k)
            k = steps.step(nc.vector.memset(lt, 0.0))
            for t in range(NC):
                k = steps.step(nc.vector.bn_aggr(mv[:, t, :], st[:, t, :]))
            dve.wait_ge(steps.sem, k)
            k = steps.step(nc.vector.tensor_scalar(lv, mv[:, :, 1], EPS, None, ALU.add))
            dve.wait_ge(steps.sem, k)
            rsqrt(dve, steps, lv, lr, lt, lm)
            steps.step(nc.vector.tensor_copy(rstd, lr))
            steps.step(nc.vector.tensor_scalar(rp1, lr, 1.0, None, ALU.add))
            nc.vector.scalar_tensor_tensor(out=nmr, in0=mv[:, :, 0], scalar=-1.0, in1=lr, op0=ALU.mult,
                                           op1=ALU.mult).then_inc(ln_ok.sem, 1)

        def dve_xl(dve, nb):
            for t in range(NC):
                dve.wait_ge(xh_ok.sem, xh_ok.at(nb, t))
                nc.vector.scalar_tensor_tensor(out=xl[:, :, t * P:(t + 1) * P], in0=bank(4 + t).rearrange("p (k n) -> p k n", k=KD),
                                               scalar=XS, in1=xh[:, :, t * P:(t + 1) * P], op0=ALU.mult,
                                               op1=ALU.subtract).then_inc(xl_ok.sem, 1)

        def heads(v):
            return v.rearrange("p (c h) -> p c h", c=NC)

        def dve_dt(dve, steps, nb):
            dve.wait_ge(pe_dt.sem, pe_dt.at(nb, 0))
            nc.vector.scalar_tensor_tensor(out=heads(dr), in0=heads(bank(6)[:, 0:W4]), scalar=f_in[:, 0:1],
                                           in1=dtb[:].unsqueeze(1).to_broadcast([P, NC, NH]), op0=ALU.mult,
                                           op1=ALU.add).then_inc(dt_raw.sem, 1)
            dve.wait_ge(dt_exp.sem, dt_exp.at(nb, 0))
            nc.vector.tensor_scalar(du, de, 1.0, None, ALU.add).then_inc(dt_u.sem, 1)
            dve.wait_ge(dt_u.sem, dt_u.at(nb, 0))
            k = steps.step(nc.vector.scalar_tensor_tensor(out=de, in0=du, scalar=-1.0, in1=de, op0=ALU.add, op1=ALU.subtract))
            k = steps.step(nc.vector.reciprocal(dm, du))
            dve.wait_ge(steps.sem, k)
            k = steps.step(nc.vector.tensor_tensor(dm, dm, de, ALU.mult))
            dve.wait_ge(dt_ln.sem, dt_ln.at(nb, 0))
            k2 = steps.step(nc.vector.scalar_tensor_tensor(out=dl, in0=dr, scalar=0.0, in1=dl, op0=ALU.max, op1=ALU.add))
            dve.wait_ge(steps.sem, k2)
            k = steps.step(nc.vector.tensor_tensor(dtv, dl, dm, ALU.subtract))
            dve.wait_ge(steps.sem, k)
            nc.vector.tensor_tensor(heads(av), heads(dtv), nega[:].unsqueeze(1).to_broadcast([P, NC, NH]),
                                    ALU.mult).then_inc(dt_a.sem, 1)

        @block.vector
        def _(dve):
            steps = Steps(dve_steps, DVE_STEPS)
            dve.wait_ge(d_con, 32)
            steps.step(nc.vector.tensor_scalar(cmean[:], ones, 1.0 / E, None, ALU.mult))
            dve.wait_ge(d_x0, 16)
            dve_ln(dve, steps, 0)
            dve.wait_ge(alog_e, 1)
            steps.step(nc.vector.tensor_scalar(nega[:], nega[:], -1.0, None, ALU.mult))
            for k in range(KD):
                dve.wait_ge(d_win[k], 16)
                s = steps.step(nc.vector.tensor_reduce(out=mx[:, k:k + 1], in_=win_raw[:, k, :], axis=AX.X, op=ALU.max,
                                                       apply_absolute_value=True))

            def to_scale(n, first, count, prev, want):
                dve.wait_ge(steps.sem, prev)
                nc.vector.tensor_reduce(out=mx[:, 24 + n:25 + n], in_=mx[:, first:first + count], axis=AX.X,
                                        op=ALU.max).then_inc(max_part, 1)
                dve.wait_ge(max_all, n + 1)
                v, q = mx[:, 28 + n:29 + n], p2[:, n:n + 1]
                k = steps.step(nc.vector.tensor_scalar(q.bitcast(I32), v.bitcast(I32), 0x7F800000, None, ALU.bitwise_and))
                dve.wait_ge(steps.sem, k)
                k = steps.step(nc.vector.tensor_scalar(q, q, 2.0 ** -20, None, ALU.max))
                dve.wait_ge(steps.sem, k)
                k = steps.step(nc.vector.reciprocal(scl[:, n:n + 1], q))
                steps.step(nc.vector.tensor_scalar(inv[:, n:n + 1], q, 2.0 ** -want, None, ALU.mult))
                dve.wait_ge(steps.sem, k)
                k = steps.step(nc.vector.tensor_scalar(scl[:, n:n + 1], scl[:, n:n + 1], 2.0 ** want, None, ALU.mult))
                dve.wait_ge(steps.sem, k)

            dve_xl(dve, 0)
            to_scale(0, 0, KD, s, 14)
            steps.step(nc.vector.tensor_scalar(f_in[:], inv[:, 0:1], 1 / XS, None, ALU.mult))
            k = steps.step(nc.vector.tensor_scalar(f_half[:], inv[:, 0:1], 0.5 / XS, None, ALU.mult))
            dve.wait_ge(steps.sem, k)
            dve.wait_ge(d_par, 16 * N_PAR)
            steps.step(nc.vector.tensor_scalar(cw[:], cw[:], f_half[:, 0:1], None, ALU.mult))
            steps.step(nc.vector.tensor_scalar(cb[:], cb[:], 0.5, None, ALU.mult)) 
            nc.vector.tensor_scalar(p2[:, 3:4], p2[:, 0:1], 1.0, None, ALU.mult).then_inc(scale_ok, 1)
            dve.wait_ge(wdt_h, 1)
            nc.vector.scalar_tensor_tensor(out=wdt_lo[:], in0=win_raw[:, :, DT:DT + NH], scalar=scl[:, 0:1], in1=wdt_hi[:],
                                           op0=ALU.mult, op1=ALU.subtract).then_inc(wdt_h, 1)
            dve_dt(dve, steps, 0)
            dve.wait_ge(d_w2, 16)
            s = steps.step(nc.vector.tensor_reduce(out=mx[:, 4:5], in_=w2a, axis=AX.XY, op=ALU.max, apply_absolute_value=True))
            for n in range(4):
                butterfly(nc.vector, dve, n, 0, D_SPLIT, bf_dve, steps if n == 0 else None, s)
            dve.wait_ge(d_wo, 16)
            for q in range(QE):
                s = steps.step(nc.vector.tensor_scalar(wo_raw[:, q, :], wo_raw[:, q, :], nw[:, q:q + 1], None, ALU.mult))
            dve.wait_ge(steps.sem, s)
            s = steps.step(nc.vector.tensor_reduce(out=mx[:, 5:6], in_=wo_raw, axis=AX.XY, op=ALU.max, apply_absolute_value=True))
            for i in range(2 * KD):
                dve.wait_ge(d_w13[i % 4], 16 * (i // 4 + 1))
                nc.vector.tensor_reduce(out=mx[:, 8 + i:9 + i], in_=w13_raw[i % 4], axis=AX.X, op=ALU.max,
                                        apply_absolute_value=True).then_inc(w13_seen, 1)
            dve.wait_ge(w13_seen, 2 * KD)
            to_scale(1, 8, 2 * KD, s, 14)
            to_scale(2, 5, 1, s, 14)
            to_scale(3, 4, 1, s, 8)
            steps.step(nc.vector.tensor_scalar(f_13[:], inv[:, 1:2], 0.5 / XS, None, ALU.mult))
            steps.step(nc.vector.tensor_scalar(f_out[:], inv[:, 2:3], 1 / XS, None, ALU.mult))
            steps.step(nc.vector.tensor_scalar(f_had[:], scl[:, 3:4], float(np.float32(1 / np.sqrt(HF))), None, ALU.mult))
            k = steps.step(nc.vector.tensor_scalar(f_w2[:], inv[:, 1:2], inv[:, 1:2], 2.0 ** 33, ALU.mult, ALU.mult))
            dve.wait_ge(steps.sem, k)
            k = steps.step(nc.vector.tensor_tensor(f_w2[:], f_w2[:], inv[:, 3:4], ALU.mult))
            dve.wait_ge(steps.sem, k)
            nc.vector.tensor_copy(p2[:, 0:1], p2[:, 1:2]).then_inc(scale_ok, 2)
            for q in range(QE):
                dve.wait_ge(wo_h, q + 1)
                k = steps.step(nc.vector.scalar_tensor_tensor(out=wo_lo[:, q, :], in0=wo_raw[:, q, :], scalar=scl[:, 2:3],
                                                              in1=wo_hi[:, q, :], op0=ALU.mult, op1=ALU.subtract))
            for j in range(JF):
                dve.wait_ge(had_hi, j + 1)
                nc.vector.scalar_tensor_tensor(out=w2p[:, j, D:2 * D], in0=bank(j % ACC_BANKS), scalar=f_had[:, 0:1],
                                               in1=w2p[:, j, 0:D], op0=ALU.mult, op1=ALU.subtract).then_inc(had_lo, 1)
            dve.wait_ge(had_lo, JF)
            dve.wait_ge(steps.sem, k)
            dve.nop().then_inc(ready, 1)
            dve.wait_ge(ready, ENGINES_READY)
            with dve.Fori(0, NB) as b:
                steps.enter(b)

                def split_lo(key):
                    p = POS[key]
                    dve.wait_ge(w_hi.sem, w_hi.at(b, p))
                    nc.vector.scalar_tensor_tensor(out=part_lo[p % PARTS], in0=raw[p % RAW], scalar=weight_scale(key),
                                                   in1=part_hi[p % PARTS], op0=ALU.mult, op1=ALU.subtract).then_inc(w_lo.sem, 1)

                def finish(key):
                    kind, i = key
                    p = POS[key]
                    src = bank(p % ACC_BANKS)
                    if kind == "C":
                        n = C_ORDER[i]
                        a = acc[n % 2]
                        dve.wait_ge(acc_ok.sem, acc_ok.at(b, n))
                        for s in range(1, TAPS):
                            ins = nc.vector.scalar_tensor_tensor(out=a[:, s:L], in0=src[:, 0:L - s],
                                                                 scalar=cw[:, i, TAPS - 1 - s:TAPS - s], in1=a[:, s:L],
                                                                 op0=ALU.mult, op1=ALU.add)
                            if s < TAPS - 1:
                                dve.wait_ge(steps.sem, steps.step(ins))
                        ins.then_inc(evac.sem, 1)
                        dve.wait_ge(tanh_ok.sem, tanh_ok.at(b, TANH[key]))
                        nc.vector.scalar_tensor_tensor(out=XT[:, i, :], in0=tb[TANH[key] % 2], scalar=1.0, in1=a,
                                                       op0=ALU.add, op1=ALU.mult).then_inc(xt_done.sem, 1)
                    elif kind == "Z":
                        dve.wait_ge(tanh_ok.sem, tanh_ok.at(b, TANH[key]))
                        nc.vector.scalar_tensor_tensor(out=gz[:, i, :], in0=tb[TANH[key] % 2], scalar=1.0, in1=src,
                                                       op0=ALU.add, op1=ALU.mult).then_inc(evac.sem, 1)
                    elif kind == "G1":
                        dve.wait_ge(tanh_ok.sem, tanh_ok.at(b, TANH[key]))
                        dve.wait_ge(hid_l.sem, hid_l.at(b, max(i - 2, -1)))
                        nc.vector.scalar_tensor_tensor(out=hs[i % 2], in0=tb[TANH[key] % 2], scalar=1.0, in1=src,
                                                       op0=ALU.add, op1=ALU.mult).then_inc(evac.sem, 1)
                    else:
                        dve.wait_ge(tile_done.sem, tile_done.at(b, p))
                        dve.wait_ge(evac.sem, evac.at(b, p - 1))
                        nc.vector.scalar_tensor_tensor(out=hs[i % 2], in0=src, scalar=2.0 ** -33 / (2 * XS * XS), in1=hs[i % 2],
                                                       op0=ALU.mult, op1=ALU.mult).then_inc(evac.sem, 1)

                k = steps.step(nc.vector.tensor_copy(rp1_cur, rp1))
                k = steps.step(nc.vector.tensor_copy(nmr_cur, nmr))
                for key in STREAM[:2]:
                    split_lo(key)
                ahead = 2
                for kind, i in SCHEDULE:
                    c = i
                    if kind in ("C", "Z", "F"):
                        for key in ([(kind, i)] if kind != "F" else [("G1", i), ("U3", i)]):
                            if ahead < NT:
                                split_lo(STREAM[ahead])
                                ahead += 1
                            finish(key)
                    elif kind == "T":
                        dve.wait_ge(pe_x.sem, pe_x.at(b, c))
                        nc.vector.tensor_tensor(Xdt.rearrange("p (h d) -> p h d", h=NH),
                                                bank(4, 2).rearrange("p (h d) -> p h d", h=NH),
                                                dtv[:, c * NH:(c + 1) * NH].unsqueeze(2).to_broadcast([P, NH, HD]),
                                                ALU.mult).then_inc(xdt_ok.sem, 1)
                        dve.wait_ge(pe_g.sem, pe_g.at(b, c))
                        nc.vector.tensor_tensor(Gm, bank(7)[:, 0:P], tri_le, ALU.mult).then_inc(gm_ok.sem, 1)
                    elif kind == "X":
                        dve.wait_ge(eexp_ok.sem, eexp_ok.at(b, c))
                        dve.wait_ge(gm_ok.sem, gm_ok.at(b, c))
                        nc.vector.tensor_tensor(Eb, Eb, Gm.unsqueeze(1).to_broadcast([P, NH, P]), ALU.mult).then_inc(m_ok.sem, 1)
                    elif kind == "S":
                        if c > 0:
                            dve.wait_ge(pe_off.sem, pe_off.at(b, c - 1))
                            dve.wait_ge(d_ecsb, (b * (NC - 1) + c) * 32)
                            nc.vector.tensor_tensor(t1, bank(6, 2), ecsb, ALU.mult).then_inc(t1_ok.sem, 1)
                        if 0 < c < NC - 1:
                            dve.wait_ge(pe_state.sem, pe_state.at(b, c))
                            dve.wait_ge(sdec_ok.sem, sdec_ok.at(b, c - 1))
                            nc.vector.tensor_tensor(state, bank(4, 2), state, ALU.add).then_inc(state_ok.sem, 1)
                    elif kind == "Y":
                        dve.wait_ge(pe_diag.sem, pe_diag.at(b, c))
                        if c > 0:
                            dve.wait_ge(t2_ok.sem, t2_ok.at(b, c - 1))
                        else:
                            dve.wait_ge(xd_ok.sem, xd_ok.at(b, c))
                        nc.vector.tensor_tensor(y, bank(6, 2), XD, ALU.add).then_inc(diag_read.sem, 1)
                        dve.wait_ge(diag_read.sem, diag_read.at(b, c))
                        y3 = y.rearrange("p (q l) -> p q l", q=QE)
                        nc.vector.scalar_tensor_tensor(out=y3, in0=y3, scalar=f_half[:, 0:1], in1=gz[:, :, c * P:(c + 1) * P],
                                                       op0=ALU.mult, op1=ALU.mult).then_inc(ygate_ok.sem, 1)
                        dve.wait_ge(sq_ok.sem, sq_ok.at(b, c))
                        nc.vector.tensor_reduce(out=sqr, in_=t1.rearrange("p (q l) -> p l q", q=QE), axis=AX.X,
                                                op=ALU.add).then_inc(sqr_ok.sem, 1)
                    elif kind == "N":
                        dve.wait_ge(pe_mean.sem, pe_mean.at(b, c))
                        nc.vector.tensor_scalar(nv, bank(4)[:, 0:P], EPS, None, ALU.add).then_inc(mean_read.sem, 1)
                        dve.wait_ge(mean_read.sem, mean_read.at(b, c))
                        rsqrt(dve, steps, nv, nr, ntmp, sqr)
                        y3 = y.rearrange("p (q l) -> p q l", q=QE)
                        nc.vector.tensor_tensor(y3, y3, nr.unsqueeze(1).to_broadcast([P, QE, P]), ALU.mult).then_inc(yn_ok.sem, 1)
                        dve.wait_ge(yh_ok.sem, yh_ok.at(b, c))
                        nc.vector.scalar_tensor_tensor(out=yl, in0=y3, scalar=XS, in1=yh, op0=ALU.mult,
                                                       op1=ALU.subtract).then_inc(yl_ok.sem, 1)
                    elif kind == "W":
                        dve.wait_ge(d_xr[c % 2], (b * (NC // 2) + (c // 2 + 1)) * 16)
                        k = steps.step(nc.vector.tensor_scalar(xr[c % 2], xr[c % 2], rp1_cur[:, c:c + 1], nmr_cur[:, c:c + 1],
                                                               ALU.mult, ALU.add))
                        dve.wait_ge(steps.sem, k)
                        dve.wait_ge(pe_wout.sem, pe_wout.at(b, c))
                        if c == 0:
                            dve.wait_ge(d_out, b * (NC * 16) + 1)
                        nc.vector.scalar_tensor_tensor(out=racc[:, c, :], in0=bank(5), scalar=f_out[:, 0:1], in1=xr[c % 2],
                                                       op0=ALU.mult, op1=ALU.add).then_inc(mamba_evac.sem, 1)
                    elif kind == "LN":
                        dve.wait_ge(d_xraw, (b + 1) * 16)
                        dve_ln(dve, steps, b + 1)
                    elif kind == "XT":
                        dve_xl(dve, b + 1)
                    elif kind == "DT":
                        dve_dt(dve, steps, b + 1)
                    elif kind == "OUT":
                        dve.wait_ge(w2_used.sem, w2_used.at(b, JF - 1))
                        dve.wait_ge(mamba_evac.sem, mamba_evac.at(b, NC - 1))
                        for t in range(NC):
                            nc.vector.scalar_tensor_tensor(out=racc[:, t, :], in0=bank(t), scalar=f_w2[:, 0:1],
                                                           in1=racc[:, t, :], op0=ALU.mult, op1=ALU.add).then_inc(ffn_evac.sem, 1)
                steps.leave()

        @block.gpsimd
        def _(pool):
            def all_max(n):
                pool.wait_ge(max_part, n + 1)
                nc.gpsimd.partition_all_reduce(mx[:, 28 + n:29 + n], mx[:, 24 + n:25 + n], P,
                                               bass.bass_isa.ReduceOp.max).then_inc(max_all, 1)
            all_max(0)
            pool.wait_ge(d_w2, 16)
            for n in range(4):
                if n == 1:
                    pool.wait_ge(bf_dve, 1)
                butterfly(nc.gpsimd, pool, n, D_SPLIT, D, bf_pool, None, None)
            for n in range(1, 4):
                all_max(n)
            pool.nop().then_inc(ready, 1)
            pool.wait_ge(ready, ENGINES_READY)
            with pool.Fori(0, NB) as b:
                for kind, i in SCHEDULE:
                    c = i
                    if kind == "F":
                        pool.wait_ge(hid_h.sem, hid_h.at(b, i))
                        nc.gpsimd.tensor_tensor(hid_lo[:, i, :], hs[i % 2], hid_hi[:, i, :], ALU.subtract).then_inc(hid_l.sem, 1)
                    elif kind == "T":
                        pool.wait_ge(d_csbc, (b * NC + (c + 1)) * 16)
                        pool.wait_ge(sums_ok.sem, sums_ok.at(b, 0))
                        pool.wait_ge(pe_diag.sem, pe_diag.at(b, c - 1))
                        nc.gpsimd.tensor_tensor(Eb, csbc, cs_s[:, c * NH:(c + 1) * NH].unsqueeze(2).to_broadcast([P, NH, P]),
                                                ALU.subtract).then_inc(esub_ok.sem, 1)
                        pool.wait_ge(esub_ok.sem, esub_ok.at(b, c))
                        nc.gpsimd.tensor_tensor(pool_mark, ones[:, 0:1], ones[:, 0:1], ALU.mult)
                        nc.gpsimd.tensor_scalar(Eb, Eb, 0.0, -3.0e38, ALU.min, ALU.max).then_inc(emin_ok.sem, 1)
                        if c < NC - 1:
                            pool.wait_ge(xdt_ok.sem, xdt_ok.at(b, c))
                            nc.gpsimd.tensor_tensor(Xdec.rearrange("p (h d) -> p h d", h=NH), Xdt.rearrange("p (h d) -> p h d", h=NH),
                                                    dec[:, c * NH:(c + 1) * NH].unsqueeze(2).to_broadcast([P, NH, HD]),
                                                    ALU.mult).then_inc(xdec_ok.sem, 1)
                    elif kind == "S" and c > 0:
                        pool.wait_ge(t1_ok.sem, t1_ok.at(b, c - 1))
                        pool.wait_ge(xd_ok.sem, xd_ok.at(b, c))
                        nc.gpsimd.tensor_tensor(XD, XD, t1, ALU.add).then_inc(t2_ok.sem, 1)
                        if c < NC - 1:
                            nc.gpsimd.tensor_tensor(state.rearrange("p (h d) -> p h d", h=NH), state.rearrange("p (h d) -> p h d", h=NH),
                                                    tot[:, c * NH:(c + 1) * NH].unsqueeze(2).to_broadcast([P, NH, HD]),
                                                    ALU.mult).then_inc(sdec_ok.sem, 1)


def constants():
    k = np.arange(P)
    bits = np.array([[bin(a & c).count("1") for c in k] for a in k])
    return np.concatenate([np.eye(P), k[:, None] <= k[None, :], k[:, None] > k[None, :],
                           np.ones((P, P)), 1.0 - 2.0 * (bits % 2)], axis=1).astype(np.float32)


def kernel(L0_attn_x, L0_attn_w_in, L0_attn_conv_w, L0_attn_conv_b, L0_attn_dt_bias, L0_attn_A_log, L0_attn_D,
           L0_attn_norm_w, L0_attn_w_out, L0_ffn_W1, L0_ffn_W2, L0_ffn_W3):
    import concourse.bacc as _bacc
    from concourse.bass_utils import run_bass_kernel_spmd as _run

    x = np.asarray(L0_attn_x)
    con = np.ascontiguousarray
    arrays = {
        "x": con(np.concatenate([x, x[:1]])),
        "w_in": con(L0_attn_w_in),
        "w1t": con(np.asarray(L0_ffn_W1).T),
        "w3t": con(np.asarray(L0_ffn_W3).T),
        "w2t": con(np.asarray(L0_ffn_W2).T),
        "w_out": con(L0_attn_w_out),
        "conv_w": con(np.asarray(L0_attn_conv_w).reshape(MC, P, TAPS).transpose(1, 0, 2)),
        "conv_b": con(np.asarray(L0_attn_conv_b).reshape(MC, P).T),
        "dt_bias": con(np.broadcast_to(np.asarray(L0_attn_dt_bias), (P, NH))),
        "a_log": con(np.broadcast_to(np.asarray(L0_attn_A_log), (P, NH))),
        "d_cols": con(np.repeat(np.asarray(L0_attn_D), HD).reshape(QE, P).T),
        "norm_w": con(np.asarray(L0_attn_norm_w).reshape(QE, P).T),
        "consts": constants(),
    }
    nc = _bacc.Bacc("TRN2", target_bir_lowering=False, num_devices=1)
    args = [nc.dram_tensor(n, a.shape, mybir.dt.from_np(a.dtype), kind="ExternalInput").ap() for n, a in arrays.items()]
    out = nc.dram_tensor("out", (NB, L, D), FP32, kind="ExternalOutput").ap()
    build(nc, *args, out)
    r = _run(nc, [arrays], core_ids=[0])
    return r.results[0]["out"]
```

```python
import numpy as np
import concourse.bass as bass
from concourse import mybir
from contextlib import ExitStack

FP32, FP16, I32 = mybir.dt.float32, mybir.dt.float16, mybir.dt.int32
ALU, ACT, AX = mybir.AluOpType, mybir.ActivationFunctionType, mybir.AxisListType

P = 128
NB, L, D = 4, 512, 512
KD = D // P
E, NH, HD, NS = 1024, 16, 64, 128
QE = E // P
CONV = E + 2 * NS
MC, MZ = CONV // P, E // P
TAPS = 4
NC = L // P
HF = 2048
JF = HF // P
EPS = 1e-5
XS = 1024.0
NT = MC + MZ + 2 * JF
RAW, PARTS, W2R = 2, 5, 4
AHEAD = 2
FREE_BANK = 3
DT = 2 * E + 2 * NS
B_TILE, C_TILE = QE, QE + 1

STEP_AT = {"T": 0, "X": 1, "S": 2, "R": 3, "Y": 4, "E": 5, "Q": 5, "N": 6, "V": 8, "W": 9}
CHUNK_EVERY = 8


def make_schedule():
    front = [("C", B_TILE), ("C", C_TILE), ("E", 0)]
    for m in range(QE):
        front += [("C", m), ("Z", m)]
    tiles = [(k, j) for j in range(JF) for k in "AU"] + [("G", j) for j in range(JF)]
    after = [[] for _ in tiles]
    before = []
    for c in range(NC):
        for step, slot in STEP_AT.items():
            n = c * CHUNK_EVERY + slot - 1
            item = (step, c + 1) if step == "E" else (step, c)
            if step == "E" and c == NC - 1:
                continue
            (after[n] if n >= 0 else before).append(item)
    after[19].append(("LN", 0))
    after[2 * JF + 2].append(("XT", 0))
    after[2 * JF + 5].append(("DT", 0))
    after[2 * JF + 8].append(("SUM", 0))
    return front + before + [x for t, a in zip(tiles, after) for x in [t] + a] + [("OUT", 0)]


SCHEDULE = make_schedule()
STREAM = [key for key in SCHEDULE if key[0] in "CZAU"]
POS = {key: n for n, key in enumerate(STREAM)}
TANH_KEYS = [k for k in STREAM if k[0] != "U"]
TANH = {key: n for n, key in enumerate(TANH_KEYS)}
NTANH = len(TANH)
C_ORDER = {key[1]: n for n, key in enumerate(k for k in STREAM if k[0] == "C")}

DVE_STEPS, ACT_STEPS = 103, 1


class Signal:

    def __init__(self, sem, per_batch, start):
        self.sem, self.per_batch, self.start = sem, per_batch, start

    def at(self, nb, i):
        assert self.start + i >= 0
        return nb * self.per_batch + (self.start + i + 1)


class Steps:

    def __init__(self, sem, per_batch):
        self.sem, self.per_batch, self.n, self.base, self.b = sem, per_batch, 0, 0, 0

    def step(self, ins):
        ins.then_inc(self.sem, 1)
        self.n += 1
        return self.b * self.per_batch + (self.base + self.n)

    def enter(self, b):
        self.base, self.n, self.b = self.n, 0, b

    def leave(self):
        assert self.n == self.per_batch, self.n


def build(nc, x, w_in, w1t, w3t, w2t, w_out, conv_w, conv_b, dt_bias, a_log, d_cols, norm_w, consts, out):
    w2_parts = nc.dram_tensor("w2_parts", (JF, P, 2 * D), FP16, kind="Internal").ap()
    cs_rows = nc.dram_tensor("cs_rows", (NB + 1, NC, NH, P), FP32, kind="Internal").ap()
    ecs_rows = nc.dram_tensor("ecs_rows", (NB + 1, NC, NH, P), FP32, kind="Internal").ap()
    ctx = ExitStack()
    with ctx:
        def sb(name, shape, dt=FP32):
            return ctx.enter_context(nc.sbuf_tensor(name, shape, dt))

        def sem(name):
            return ctx.enter_context(nc.semaphore(name))

        con = sb("con", [P, 4 * P])
        ident, tri_le, tri_gt, ones = (con[:, i * P:(i + 1) * P] for i in range(4))
        cmean = sb("cmean", [P, P])
        wo_hi, wo_lo = sb("wo_hi", [P, QE, D], FP16), sb("wo_lo", [P, QE, D], FP16)
        xh, xl = sb("xh", [P, KD, L], FP16), sb("xl", [P, KD, L], FP16)
        wdt_hi, wdt_lo = sb("wdt_hi", [P, KD, NH], FP16), sb("wdt_lo", [P, KD, NH], FP16)
        cw, cb = sb("cw", [P, MC, TAPS]), sb("cb", [P, MC])
        dtb, nega, dcol, nw = sb("dtb", [P, NH]), sb("nega", [P, NH]), sb("dcol", [P, QE]), sb("nw", [P, QE])
        scl, inv, mx = sb("scl", [P, 4]), sb("inv", [P, 4]), sb("mx", [P, 32])
        p2 = sb("p2", [P, 4])
        pool_mark = mx[:, 23:24]
        f_in, f_half, f_13, f_out, f_w2, f_had = (sb(n, [P, 1]) for n in ("f_in", "f_half", "f_13", "f_out", "f_w2", "f_had"))

        arena_words = 46150
        STAGED = KD * (DT + NH) + 2 * JF * D + QE * D + 4 * HF + P
        arena = sb("arena", [P, arena_words])
        used = [0]

        def view(words, dt=FP32):
            a = arena[:, used[0]:used[0] + words]
            used[0] += words
            return a if dt == FP32 else a.bitcast(dt)

        def cut(v, n):
            return v.rearrange("p (a b) -> p a b", a=n)

        hid_hi, hid_lo = cut(view(JF * L // 2, FP16), JF), cut(view(JF * L // 2, FP16), JF)
        XT = cut(view(MC * L), MC)
        gz = cut(view(MZ * L), MZ)
        csbc, Eb = cut(view(NH * P), NH), cut(view(NH * P), NH)
        Xdt, Xdec, ecsb, state, t1, XD, y = (view(E) for _ in range(7))
        Bs, Gm = view(P), view(P)
        sqr, nv, nr, ntmp = (view(P) for _ in range(4))
        yh, yl = cut(view(E // 2, FP16), QE), cut(view(E // 2, FP16), QE)
        raw = [cut(view(KD * P), KD) for _ in range(RAW)]
        part_hi = [cut(view(KD * P // 2, FP16), KD) for _ in range(PARTS)]
        part_lo = [cut(view(KD * P // 2, FP16), KD) for _ in range(PARTS)]
        tb, acc, hs = ([view(L) for _ in range(2)] for _ in range(3))
        w2s = [cut(view(D, FP16), 2) for _ in range(W2R)]
        assert used[0] >= STAGED
        xraw = cut(view(NC * D), NC)
        racc = cut(view(NC * D), NC)
        xr = [view(D) for _ in range(2)]
        W4 = NC * NH
        dr, de, du, dl, dm, dtv, av, cs_s, dec, tot = (view(W4) for _ in range(10))
        csT, ecsT = view(L)[0:NH, :], view(L)[0:NH, :]
        st = cut(view(NC * 6), NC)
        mv = cut(view(NC * 2), NC)
        lv, lr, lt, lm = (view(NC) for _ in range(4))
        rstd, nmr, rp1, nmr_cur, rp1_cur = (view(NC) for _ in range(5))

        used_p = [0]

        def stage(words):
            a = arena[:, used_p[0]:used_p[0] + words]
            used_p[0] += words
            return a
        win_raw = cut(stage(KD * (DT + NH)), KD)
        w2a, w2b = cut(stage(JF * D), JF), cut(stage(JF * D), JF)
        wo_raw = cut(stage(QE * D), QE)
        w13_raw = [stage(HF) for _ in range(4)]
        hadam = stage(P)
        assert used_p[0] == STAGED
        w2p = w2b.rearrange("p a b -> p (a b)").bitcast(FP16).rearrange("p (a c) -> p a c", a=JF)

        ps = ctx.enter_context(nc.psum_tensor("ps", [P, 8 * L], FP32))

        def bank(i, n=1):
            return ps[:, i * L:(i + n) * L]

        d_con, d_par, d_x0 = sem("d_con"), sem("d_par"), sem("d_x0")
        d_win = [sem(f"d_win{k}") for k in range(KD)]
        d_wo, d_w2 = sem("d_wo"), sem("d_w2")
        d_w13 = [sem(f"d_w13_{k}") for k in range(4)]
        d_w2st = sem("d_w2st")
        d_raw = [sem(f"d_raw{i}") for i in range(RAW)]
        d_w2s = [sem(f"d_w2s{i}") for i in range(W2R)]
        d_xraw, d_cst, d_csbc, d_ecsb, d_out = sem("d_xraw"), sem("d_cst"), sem("d_csbc"), sem("d_ecsb"), sem("d_out")
        d_xr = [sem(f"d_xr{i}") for i in range(2)]
        max_part, max_all, scale_ok = sem("max_part"), sem("max_all"), sem("scale_ok")
        w13_seen, wo_scaled = sem("w13_seen"), sem("wo_scaled")
        wdt_h, wo_h, alog_e = sem("wdt_h"), sem("wo_h"), sem("alog_e")
        bf_dve, bf_pool, had_done, had_hi, had_lo = sem("bf_dve"), sem("bf_pool"), sem("had_done"), sem("had_hi"), sem("had_lo")
        ready = sem("ready")
        signals = []

        def signal(name, per_batch, start=0):
            signals.append(Signal(sem(name), per_batch, start))
            return signals[-1]

        w_hi = signal("w_hi", NT)
        w_lo = signal("w_lo", NT, RAW)
        tile_done = signal("tile_done", NT, PARTS)
        evac = signal("evac", NT, 1)
        acc_ok = signal("acc_ok", MC)
        tanh_ok = signal("tanh_ok", NTANH)
        xt_done = signal("xt_done", MC, 1)
        hid_h = signal("hid_h", JF)
        hid_l = signal("hid_l", JF, 1)
        w2_used = signal("w2_used", JF, W2R)
        ffn_evac = signal("ffn_evac", NC, NC)
        pe_x = signal("pe_x", NC)
        pe_b = signal("pe_b", NC)
        pe_g = signal("pe_g", NC)
        pe_off = signal("pe_off", NC - 1)
        pe_state = signal("pe_state", NC - 1)
        pe_diag = signal("pe_diag", NC, 1)
        pe_mean = signal("pe_mean", NC)
        pe_wout = signal("pe_wout", NC, 1)
        gm_ok = signal("gm_ok", NC)
        xdt_ok = signal("xdt_ok", NC)
        bs_ok = signal("bs_ok", NC)
        xd_ok = signal("xd_ok", NC)
        xdec_ok = signal("xdec_ok", NC - 1)
        esub_ok = signal("esub_ok", NC, 1)
        emin_ok = signal("emin_ok", NC)
        eexp_ok = signal("eexp_ok", NC)
        m_ok = signal("m_ok", NC)
        t1_ok = signal("t1_ok", NC - 1, 1)
        t2_ok = signal("t2_ok", NC - 1)
        state0_ok = signal("state0_ok", 1)
        sdec_ok = signal("sdec_ok", NC - 2)
        state_ok = signal("state_ok", NC - 2)
        diag_read = signal("diag_read", NC, 1)
        ygate_ok = signal("ygate_ok", NC)
        sq_ok = signal("sq_ok", NC)
        sqr_ok = signal("sqr_ok", NC)
        mean_read = signal("mean_read", NC)
        yn_ok = signal("yn_ok", NC)
        yh_ok = signal("yh_ok", NC)
        yl_ok = signal("yl_ok", NC)
        mamba_evac = signal("mamba_evac", NC, 1)
        ln_ok = signal("ln_ok", 1)
        xn_ok = signal("xn_ok", NC)
        pe_xt = signal("pe_xt", NC)
        xh_ok = signal("xh_ok", NC)
        xl_ok = signal("xl_ok", NC)
        pe_dt = signal("pe_dt", 1)
        dt_raw = signal("dt_raw", 1)
        dt_exp = signal("dt_exp", 1)
        dt_u = signal("dt_u", 1)
        dt_ln = signal("dt_ln", 1)
        dt_a = signal("dt_a", 1)
        pe_sums = signal("pe_sums", 1)
        pe_cst = signal("pe_cst", 1)
        sums_ok = signal("sums_ok", 1)
        cst_ok = signal("cst_ok", 1)
        ecst_ok = signal("ecst_ok", 1)
        dve_steps, act_steps = sem("dve_steps"), sem("act_steps")
        ENGINES_READY = 5
        N_PAR = 6

        def weight_tile(key, engine_view=None):
            kind, i = key
            if kind == "C":
                src, col = w_in, E + i * P
            elif kind == "Z":
                src, col = w_in, i * P
            elif kind == "A":
                src, col = w1t, i * P
            else:
                src, col = w3t, i * P
            return src.rearrange("(k p) n -> p k n", p=P)[:, :, col:col + P]

        def weight_scale(key):
            return scl[:, 0:1] if key[0] in "CZ" else scl[:, 1:2]

        def tile_bank(p):
            return bank(4 + p if p < 2 else (p - 2) % 3)

        def out_bank(c):
            return (bank(FREE_BANK), bank(FREE_BANK)) if c < NC - 1 else (bank(4), bank(5))

        block = ctx.enter_context(nc.Block())

        D_SPLIT = 352

        def butterfly(eng, e, n, lo, hi, done, steps, s):
            h = 1 << n
            src, dst = (w2a, w2b) if n % 2 == 0 else (w2b, w2a)
            if n > 0:
                e.wait_ge(done, n)
            if n == 0 and lo > 0:
                pass
            v = src[:, :, lo:hi].rearrange("p (g two h) d -> p g two h d", two=2, h=h)
            w = dst[:, :, lo:hi].rearrange("p (g two h) d -> p g two h d", two=2, h=h)
            for g in range(JF // (2 * h)):
                eng.tensor_tensor(w[:, g, 0], v[:, g, 0], v[:, g, 1], ALU.add)
                last = eng.tensor_tensor(w[:, g, 1], v[:, g, 0], v[:, g, 1], ALU.subtract)
            last.then_inc(done, 1)

        def load_tile(sp, b, p):
            sp.wait_ge(w_lo.sem, w_lo.at(b, p - RAW))
            sp.dma_start(raw[p % RAW], weight_tile(STREAM[p % NT])).then_inc(d_raw[p % RAW], 16)

        def load_w2(sp, b, j):
            sp.wait_ge(w2_used.sem, w2_used.at(b, j - W2R))
            sp.dma_start(w2s[j % W2R], w2_parts[j].rearrange("p (a d) -> p a d", a=2)).then_inc(d_w2s[j % W2R], 16)

        @block.sync
        def _(sp):
            for s in signals:
                if s.start:
                    sp.sem_inc(s.sem, s.start)
            sp.sem_inc(d_out, 1)
            sp.dma_start(con[:], consts[:, 0:4 * P]).then_inc(d_con, 16)
            sp.dma_start(hadam, consts[:, 4 * P:5 * P]).then_inc(d_con, 16)
            for dst, src in ((cw, conv_w), (cb, conv_b), (dtb, dt_bias), (nega, a_log), (dcol, d_cols), (nw, norm_w)):
                sp.dma_start(dst[:], src).then_inc(d_par, 16)
            sp.dma_start(xraw, x[0].rearrange("(t p) d -> p t d", p=P)).then_inc(d_x0, 16)
            win_v = w_in.rearrange("(k p) n -> p k n", p=P)
            for k in range(KD):
                sp.dma_start(win_raw[:, k, :], win_v[:, k, :]).then_inc(d_win[k], 16)
            sp.dma_start(w2a, w2t.rearrange("(j p) d -> p j d", p=P)).then_inc(d_w2, 16)
            sp.dma_start(wo_raw, w_out.rearrange("(q p) d -> p q d", p=P)).then_inc(d_wo, 16)
            for i in range(2 * KD):
                src = (w1t, w3t)[i // KD].rearrange("(k p) n -> p k n", p=P)[:, i % KD, :]
                if i >= 4:
                    sp.wait_ge(w13_seen, i - 3)
                sp.dma_start(w13_raw[i % 4], src).then_inc(d_w13[i % 4], 16)
            for j in range(JF):
                sp.wait_ge(had_lo, j + 1)
                sp.dma_start(w2_parts[j], w2p[:, j, :]).then_inc(d_w2st, 16)
            sp.wait_ge(d_w2st, 16 * JF)
            sp.nop().then_inc(ready, 1)
            sp.wait_ge(ready, ENGINES_READY)
            for p in range(AHEAD):
                load_tile(sp, 0, p)
            with sp.Fori(0, NB) as b:
                for kind, i in SCHEDULE:
                    if kind in "CZAU":
                        load_tile(sp, b, POS[kind, i] + AHEAD)
                    if kind == "A" and i == 4:
                        sp.wait_ge(pe_xt.sem, pe_xt.at(b, NC - 1))
                        sp.dma_start(xraw, x[b + 1].rearrange("(t p) d -> p t d", p=P)).then_inc(d_xraw, 16)
                    if kind == "U" and i >= JF - W2R:
                        load_w2(sp, b, i - (JF - W2R))
                    if kind == "G" and i < JF - W2R:
                        load_w2(sp, b, i + W2R)
                    if kind == "OUT":
                        for t in range(NC):
                            sp.wait_ge(ffn_evac.sem, ffn_evac.at(b, t))
                            sp.dma_start(out[b, t * P:(t + 1) * P, :], racc[:, t, :]).then_inc(d_out, 16)
            for i in range(RAW):
                sp.wait_ge(d_raw[i], (NB * (NT // RAW) + 1) * 16)
            sp.wait_ge(d_out, NB * NC * 16 + 1)

        def three(out_ap, lhs, rhs, n, last):
            for i in range(n):
                for s, (a, c) in enumerate(((0, 0), (0, 1), (1, 0))):
                    ins = nc.tensor.matmul(out_ap, lhs(i, a), rhs(i, c), start=(i == 0 and s == 0),
                                           stop=(i == n - 1 and s == 2))
            return ins

        def pe_transposes(pe, nb, loop):
            for t in range(NC):
                pe.wait_ge(xn_ok.sem, xn_ok.at(nb, t))
                if t >= 2:
                    pe.wait_ge(xl_ok.sem, xl_ok.at(nb, t - 2))
                for k in range(KD):
                    ins = nc.tensor.transpose(bank(6 + t % 2)[:, k * P:(k + 1) * P], xraw[:, t, k * P:(k + 1) * P], ident)
                ins.then_inc(pe_xt.sem, 1)

        def pe_dt_proj(pe, nb):
            pe.wait_ge(xl_ok.sem, xl_ok.at(nb, NC - 1))
            xs, ws = (xh, xl), (wdt_hi, wdt_lo)
            for t in range(NC):
                ins = three(bank(6)[:, t * NH:(t + 1) * NH], lambda k, a: xs[a][:, k, t * P:(t + 1) * P],
                            lambda k, c: ws[c][:, k, :], KD, None)
            ins.then_inc(pe_dt.sem, 1)

        def pe_cumsums(pe, nb):
            pe.wait_ge(dt_a.sem, dt_a.at(nb, 0))
            nc.tensor.matmul(bank(7)[:, 0:W4], tri_le, av, start=True, stop=True)
            nc.tensor.matmul(bank(7)[:, W4:2 * W4], tri_gt, av, start=True, stop=True)
            nc.tensor.matmul(bank(7)[:, 2 * W4:3 * W4], ones, av, start=True, stop=True).then_inc(pe_sums.sem, 1)
            for t in range(NC):
                ins = nc.tensor.matmul(bank(6)[0:NH, t * P:(t + 1) * P], av[:, t * NH:(t + 1) * NH], tri_le,
                                       start=True, stop=True)
            ins.then_inc(pe_cst.sem, 1)

        @block.tensor
        def _(pe):
            pe.wait_ge(d_con, 32)
            pe_transposes(pe, 0, False)
            pe.wait_ge(wdt_h, 2)
            pe_dt_proj(pe, 0)
            pe_cumsums(pe, 0)
            for j in range(JF):
                if j == 0:
                    pe.wait_ge(bf_dve, 4)
                    pe.wait_ge(bf_pool, 4)
                else:
                    pass
                if j >= 4:
                    pe.wait_ge(had_lo, j - 4 + 1)
                nc.tensor.matmul(bank(j % 4), hadam, w2a[:, j, :], start=True, stop=True).then_inc(had_done, 1)
            pe.wait_ge(had_lo, JF)
            pe.nop().then_inc(ready, 1)
            pe.wait_ge(ready, ENGINES_READY)
            xs, wos = (xh, xl), (wo_hi, wo_lo)
            with pe.Fori(0, NB) as b:
                def project(key):
                    p = POS[key]
                    pe.wait_ge(w_lo.sem, w_lo.at(b, p))
                    if p >= 5:
                        pe.wait_ge(evac.sem, evac.at(b, p - 3))
                    elif p >= 2:
                        pe.wait_ge(ffn_evac.sem, ffn_evac.at(b, p - 2 - NC))
                    w = (part_hi[p % PARTS], part_lo[p % PARTS])
                    three(tile_bank(p), lambda k, a: w[a][:, k, :], lambda k, c: xs[c][:, k, :], KD,
                          None).then_inc(tile_done.sem, 1)

                for kind, i in SCHEDULE:
                    c = i
                    cols = slice(c * P, (c + 1) * P) if kind in "TXSYNW" else None
                    if kind in "CZAU":
                        project((kind, i))
                    elif kind == "T":
                        pe.wait_ge(xt_done.sem, xt_done.at(b, MC - 1))
                        if c == 0:
                            pe.wait_ge(evac.sem, evac.at(b, 1))
                            pe.wait_ge(ecst_ok.sem, ecst_ok.at(b, 0))
                        else:
                            if c == 1:
                                pe.wait_ge(state0_ok.sem, state0_ok.at(b, 0))
                            else:
                                pe.wait_ge(state_ok.sem, state_ok.at(b, c - 2))
                            pe.wait_ge(diag_read.sem, diag_read.at(b, c - 1))
                        for q in range(QE):
                            ins = nc.tensor.transpose(bank(4, 2)[:, q * P:(q + 1) * P], XT[:, q, cols], ident)
                        ins.then_inc(pe_x.sem, 1)
                        nc.tensor.transpose(bank(6)[:, 0:P], XT[:, B_TILE, cols], ident).then_inc(pe_b.sem, 1)
                        nc.tensor.matmul(bank(7)[:, 0:P], XT[:, B_TILE, cols], XT[:, C_TILE, cols],
                                         start=True, stop=True).then_inc(pe_g.sem, 1)
                    elif kind == "S":
                        pe.wait_ge(bs_ok.sem, bs_ok.at(b, c))
                        pe.wait_ge(gm_ok.sem, gm_ok.at(b, c))
                        if c > 0:
                            if c == 1:
                                pe.wait_ge(state0_ok.sem, state0_ok.at(b, 0))
                            else:
                                pe.wait_ge(state_ok.sem, state_ok.at(b, c - 2))
                            for q in range(QE):
                                ins = nc.tensor.matmul(bank(6, 2)[:, q * P:(q + 1) * P], state[:, q * P:(q + 1) * P],
                                                       XT[:, C_TILE, cols], start=True, stop=True)
                            ins.then_inc(pe_off.sem, 1)
                        if c < NC - 1:
                            pe.wait_ge(xdec_ok.sem, xdec_ok.at(b, c))
                            for h in range(2):
                                ins = nc.tensor.matmul(bank(4 + h), Bs, Xdec[:, h * L:(h + 1) * L], start=True, stop=True)
                            ins.then_inc(pe_state.sem, 1)
                    elif kind == "Y":
                        pe.wait_ge(m_ok.sem, m_ok.at(b, c))
                        if c > 0:
                            pe.wait_ge(t1_ok.sem, t1_ok.at(b, c - 1))
                        for h in range(NH):
                            r, q = HD * (h % 2), h // 2
                            ins = nc.tensor.matmul(bank(6, 2)[r:r + HD, q * P:(q + 1) * P], Xdt[:, h * HD:(h + 1) * HD],
                                                   Eb[:, h, :], start=True, stop=True)
                        ins.then_inc(pe_diag.sem, 1)
                    elif kind == "N":
                        pe.wait_ge(sqr_ok.sem, sqr_ok.at(b, c))
                        if c == 0:
                            pe.wait_ge(ffn_evac.sem, ffn_evac.at(b, FREE_BANK - NC))
                        else:
                            pe.wait_ge(mamba_evac.sem, mamba_evac.at(b, c - 1))
                        nc.tensor.matmul(out_bank(c)[0][:, 0:P], cmean[:], sqr, start=True, stop=True).then_inc(pe_mean.sem, 1)
                    elif kind == "W":
                        pe.wait_ge(yl_ok.sem, yl_ok.at(b, c))
                        ys = (yh, yl)
                        three(out_bank(c)[1], lambda q, a: ys[a][:, q, :], lambda q, d: wos[d][:, q, :], QE,
                              None).then_inc(pe_wout.sem, 1)
                    elif kind == "G":
                        pe.wait_ge(hid_l.sem, hid_l.at(b, i))
                        pe.wait_ge(d_w2s[i % W2R], (b * (JF // W2R) + (i // W2R + 1)) * 16)
                        if i == 0:
                            pe.wait_ge(evac.sem, evac.at(b, NT - 1))
                            pe.wait_ge(mamba_evac.sem, mamba_evac.at(b, NC - 2))
                        hw = (hid_hi, hid_lo)
                        for t in range(NC):
                            for s, (a, d) in enumerate(((0, 0), (0, 1), (1, 0))):
                                ins = nc.tensor.matmul(bank(t), hw[a][:, i, t * P:(t + 1) * P], w2s[i % W2R][:, d, :],
                                                       start=(i == 0 and s == 0), stop=(i == JF - 1 and s == 2),
                                                       skip_group_check=True)
                        ins.then_inc(w2_used.sem, 1)
                    elif kind == "XT":
                        pe.wait_ge(diag_read.sem, diag_read.at(b, NC - 1))
                        pe_transposes(pe, b + 1, True)
                    elif kind == "DT":
                        pe_dt_proj(pe, b + 1)
                    elif kind == "SUM":
                        pe_cumsums(pe, b + 1)

        def act_xn(act, nb):
            act.wait_ge(ln_ok.sem, ln_ok.at(nb, 0))
            for t in range(NC):
                nc.scalar.activation(xraw[:, t, :], xraw[:, t, :], ACT.Identity, bias=nmr[:, t:t + 1],
                                     scale=rstd[:, t:t + 1]).then_inc(xn_ok.sem, 1)

        def act_xh(act, nb):
            for t in range(NC):
                act.wait_ge(pe_xt.sem, pe_xt.at(nb, t))
                nc.scalar.activation(xh[:, :, t * P:(t + 1) * P], bank(6 + t % 2).rearrange("p (k n) -> p k n", k=KD),
                                     ACT.Copy, scale=XS).then_inc(xh_ok.sem, 1)

        def act_dt(act, steps, nb):
            act.wait_ge(dt_raw.sem, dt_raw.at(nb, 0))
            k = steps.step(nc.scalar.activation(de, dr, ACT.Abs))
            act.wait_ge(steps.sem, k)
            nc.scalar.activation(de, de, ACT.Exp, scale=-1.0).then_inc(dt_exp.sem, 1)
            act.wait_ge(dt_u.sem, dt_u.at(nb, 0))
            nc.scalar.activation(dl, du, ACT.Ln).then_inc(dt_ln.sem, 1)

        def act_sums(act, steps, nb):
            act.wait_ge(pe_sums.sem, pe_sums.at(nb, 0))
            nc.scalar.activation(cs_s, bank(7)[:, 0:W4], ACT.Copy)
            nc.scalar.activation(dec, bank(7)[:, W4:2 * W4], ACT.Exp)
            nc.scalar.activation(tot, bank(7)[:, 2 * W4:3 * W4], ACT.Exp).then_inc(sums_ok.sem, 1)
            act.wait_ge(pe_cst.sem, pe_cst.at(nb, 0))
            if not isinstance(nb, int):
                act.wait_ge(d_cst, nb * 32)
            nc.scalar.activation(csT, bank(6)[0:NH, :], ACT.Copy).then_inc(cst_ok.sem, 1)
            nc.scalar.activation(ecsT, bank(6)[0:NH, :], ACT.Exp).then_inc(ecst_ok.sem, 1)
            act.wait_ge(cst_ok.sem, cst_ok.at(nb, 0))
            act.dma_start(cs_rows[nb].rearrange("c h l -> h c l"), csT.rearrange("h (c l) -> h c l", c=NC)).then_inc(d_cst, 16)
            act.wait_ge(ecst_ok.sem, ecst_ok.at(nb, 0))
            act.dma_start(ecs_rows[nb].rearrange("c h l -> h c l"), ecsT.rearrange("h (c l) -> h c l", c=NC)).then_inc(d_cst, 16)

        @block.scalar
        def _(act):
            steps = Steps(act_steps, ACT_STEPS)
            act.wait_ge(d_par, 16 * N_PAR)
            nc.scalar.activation(nega[:], nega[:], ACT.Exp).then_inc(alog_e, 1)
            act_xn(act, 0)
            act_xh(act, 0)
            act.wait_ge(scale_ok, 1)
            nc.scalar.activation(wdt_hi[:], win_raw[:, :, DT:DT + NH], ACT.Copy, scale=scl[:, 0:1]).then_inc(wdt_h, 1)
            act_dt(act, steps, 0)
            act_sums(act, steps, 0)
            act.wait_ge(scale_ok, 3)
            for q in range(QE):
                nc.scalar.activation(wo_hi[:, q, :], wo_raw[:, q, :], ACT.Copy, scale=scl[:, 2:3]).then_inc(wo_h, 1)
            for j in range(JF):
                act.wait_ge(had_done, j + 1)
                if j == 0:
                    act.wait_ge(bf_dve, 4)
                    act.wait_ge(bf_pool, 4)
                nc.scalar.activation(w2p[:, j, 0:D], bank(j % 4), ACT.Copy, scale=f_had[:, 0:1]).then_inc(had_hi, 1)
            act.wait_ge(had_hi, JF)
            act.nop().then_inc(ready, 1)
            act.wait_ge(ready, ENGINES_READY)
            def split_hi(b, p):
                act.wait_ge(d_raw[p % RAW], (b * (NT // RAW) + (p // RAW + 1)) * 16)
                act.wait_ge(tile_done.sem, tile_done.at(b, p - PARTS))
                nc.scalar.activation(part_hi[p % PARTS], raw[p % RAW], ACT.Copy,
                                     scale=weight_scale(STREAM[p % NT])).then_inc(w_hi.sem, 1)

            for p in range(AHEAD):
                split_hi(0, p)
            with act.Fori(0, NB) as b:
                steps.enter(b)

                def tanh_slot(key):
                    n = TANH[key]
                    if n < 2:
                        act.wait_ge(evac.sem, evac.at(b, -1))
                        return tb[n % 2]
                    kind, i = TANH_KEYS[n - 2]
                    if kind == "C":
                        act.wait_ge(xt_done.sem, xt_done.at(b, C_ORDER[i]))
                    else:
                        act.wait_ge(evac.sem, evac.at(b, POS[kind, i]))
                    return tb[n % 2]

                def finish(key):
                    kind, i = key
                    p = POS[key]
                    src = tile_bank(p)
                    if kind == "C":
                        n = C_ORDER[i]
                        act.wait_ge(tile_done.sem, tile_done.at(b, p))
                        act.wait_ge(xt_done.sem, xt_done.at(b, max(n - 2, -1)))
                        nc.scalar.activation(acc[n % 2], src, ACT.Identity, scale=cw[:, i, TAPS - 1:TAPS],
                                             bias=cb[:, i:i + 1]).then_inc(acc_ok.sem, 1)
                        slot = tanh_slot(key)
                        act.wait_ge(evac.sem, evac.at(b, p))
                        nc.scalar.activation(slot, acc[n % 2], ACT.Tanh).then_inc(tanh_ok.sem, 1)
                    elif kind in "ZA":
                        slot = tanh_slot(key)
                        act.wait_ge(tile_done.sem, tile_done.at(b, p))
                        nc.scalar.activation(slot, src, ACT.Tanh, scale=(f_half if kind == "Z" else f_13)[:, 0:1]).then_inc(tanh_ok.sem, 1)
                    else:
                        if i == 0:
                            act.wait_ge(w2_used.sem, w2_used.at(b, -1))
                        act.wait_ge(evac.sem, evac.at(b, p))
                        nc.scalar.activation(hid_hi[:, i, :], hs[i % 2], ACT.Copy).then_inc(hid_h.sem, 1)

                for kind, i in SCHEDULE:
                    c = i
                    if kind in "CZAU":
                        split_hi(b, POS[kind, i] + AHEAD)
                        finish((kind, i))
                    elif kind == "E":
                        act.wait_ge(d_cst, (b + 1) * 32)
                        act.wait_ge(esub_ok.sem, esub_ok.at(b, c - 1))
                        act.dma_start(csbc.rearrange("p h l -> p (h l)"),
                                      cs_rows[b, c].rearrange("h l -> (h l)").partition_broadcast(P)).then_inc(d_csbc, 16)
                        if c > 0:
                            act.wait_ge(t1_ok.sem, t1_ok.at(b, c - 2))
                            for r in range(2):
                                act.dma_start(ecsb[HD * r:HD * r + HD, :].rearrange("p (q l) -> p q l", q=QE),
                                              ecs_rows[b, c].rearrange("(q r) l -> r q l", r=2)[r].partition_broadcast(HD)).then_inc(d_ecsb, 16)
                    elif kind == "T":
                        act.wait_ge(mamba_evac.sem, mamba_evac.at(b, max(c - 2, -1)))
                        act.dma_start(xr[c % 2], x[b, c * P:(c + 1) * P, :]).then_inc(d_xr[c % 2], 16)
                        act.wait_ge(pe_b.sem, pe_b.at(b, c))
                        nc.scalar.activation(Bs, bank(6)[:, 0:P], ACT.Copy).then_inc(bs_ok.sem, 1)
                        act.wait_ge(diag_read.sem, diag_read.at(b, c - 1))
                        for q in range(QE):
                            ins = nc.scalar.activation(XD[:, q * P:(q + 1) * P], XT[:, q, c * P:(c + 1) * P], ACT.Copy,
                                                       scale=dcol[:, q:q + 1])
                        ins.then_inc(xd_ok.sem, 1)
                    elif kind == "X":
                        act.wait_ge(emin_ok.sem, emin_ok.at(b, c))
                        nc.scalar.activation(Eb, Eb, ACT.Exp).then_inc(eexp_ok.sem, 1)
                    elif kind == "S":
                        if c == 0:
                            act.wait_ge(pe_state.sem, pe_state.at(b, 0))
                            nc.scalar.activation(state, bank(4, 2), ACT.Copy).then_inc(state0_ok.sem, 1)
                    elif kind == "Y":
                        act.wait_ge(ygate_ok.sem, ygate_ok.at(b, c))
                        nc.scalar.activation(t1, y, ACT.Square).then_inc(sq_ok.sem, 1)
                    elif kind == "N":
                        act.wait_ge(yn_ok.sem, yn_ok.at(b, c))
                        act.wait_ge(pe_wout.sem, pe_wout.at(b, c - 1))
                        nc.scalar.activation(yh, y.rearrange("p (q l) -> p q l", q=QE), ACT.Copy, scale=XS).then_inc(yh_ok.sem, 1)
                    elif kind == "LN":
                        act_xn(act, b + 1)
                    elif kind == "XT":
                        act_xh(act, b + 1)
                    elif kind == "DT":
                        act_dt(act, steps, b + 1)
                    elif kind == "SUM":
                        act_sums(act, steps, b + 1)
                steps.leave()
            act.wait_ge(d_cst, (NB + 1) * 32)

        def rsqrt(dve, steps, v, r, tmp, vh):
            k = steps.step(nc.vector.tensor_scalar(tmp.bitcast(I32), v.bitcast(I32), 1, None, ALU.logical_shift_right))
            steps.step(nc.vector.tensor_scalar(vh, v, -0.5, None, ALU.mult))
            dve.wait_ge(steps.sem, k)
            k = steps.step(nc.vector.tensor_scalar(r.bitcast(I32), tmp.bitcast(I32), -1, 0x5F3759DF, ALU.mult, ALU.add))
            for _ in range(3):
                dve.wait_ge(steps.sem, k)
                k = steps.step(nc.vector.tensor_tensor(tmp, r, r, ALU.mult))
                dve.wait_ge(steps.sem, k)
                k = steps.step(nc.vector.tensor_tensor(tmp, tmp, vh, ALU.mult))
                dve.wait_ge(steps.sem, k)
                k = steps.step(nc.vector.scalar_tensor_tensor(out=r, in0=tmp, scalar=1.5, in1=r, op0=ALU.add, op1=ALU.mult))
            dve.wait_ge(steps.sem, k)

        def dve_ln(dve, steps, nb):
            for t in range(NC):
                k = steps.step(nc.vector.bn_stats(st[:, t, :], xraw[:, t, :]))
            dve.wait_ge(steps.sem, k)
            k = steps.step(nc.vector.memset(lt, 0.0))
            for t in range(NC):
                k = steps.step(nc.vector.bn_aggr(mv[:, t, :], st[:, t, :]))
            dve.wait_ge(steps.sem, k)
            k = steps.step(nc.vector.tensor_scalar(lv, mv[:, :, 1], EPS, None, ALU.add))
            dve.wait_ge(steps.sem, k)
            rsqrt(dve, steps, lv, lr, lt, lm)
            steps.step(nc.vector.tensor_copy(rstd, lr))
            steps.step(nc.vector.tensor_scalar(rp1, lr, 1.0, None, ALU.add))
            nc.vector.scalar_tensor_tensor(out=nmr, in0=mv[:, :, 0], scalar=-1.0, in1=lr, op0=ALU.mult,
                                           op1=ALU.mult).then_inc(ln_ok.sem, 1)

        def dve_xl(dve, nb):
            for t in range(NC):
                dve.wait_ge(xh_ok.sem, xh_ok.at(nb, t))
                nc.vector.scalar_tensor_tensor(out=xl[:, :, t * P:(t + 1) * P], in0=bank(6 + t % 2).rearrange("p (k n) -> p k n", k=KD),
                                               scalar=XS, in1=xh[:, :, t * P:(t + 1) * P], op0=ALU.mult,
                                               op1=ALU.subtract).then_inc(xl_ok.sem, 1)

        def heads(v):
            return v.rearrange("p (c h) -> p c h", c=NC)

        def dve_dt(dve, steps, nb):
            dve.wait_ge(pe_dt.sem, pe_dt.at(nb, 0))
            nc.vector.scalar_tensor_tensor(out=heads(dr), in0=heads(bank(6)[:, 0:W4]), scalar=f_in[:, 0:1],
                                           in1=dtb[:].unsqueeze(1).to_broadcast([P, NC, NH]), op0=ALU.mult,
                                           op1=ALU.add).then_inc(dt_raw.sem, 1)
            dve.wait_ge(dt_exp.sem, dt_exp.at(nb, 0))
            nc.vector.tensor_scalar(du, de, 1.0, None, ALU.add).then_inc(dt_u.sem, 1)
            dve.wait_ge(dt_u.sem, dt_u.at(nb, 0))
            k = steps.step(nc.vector.scalar_tensor_tensor(out=de, in0=du, scalar=-1.0, in1=de, op0=ALU.add, op1=ALU.subtract))
            k = steps.step(nc.vector.reciprocal(dm, du))
            dve.wait_ge(steps.sem, k)
            k = steps.step(nc.vector.tensor_tensor(dm, dm, de, ALU.mult))
            dve.wait_ge(dt_ln.sem, dt_ln.at(nb, 0))
            k2 = steps.step(nc.vector.scalar_tensor_tensor(out=dl, in0=dr, scalar=0.0, in1=dl, op0=ALU.max, op1=ALU.add))
            dve.wait_ge(steps.sem, k2)
            k = steps.step(nc.vector.tensor_tensor(dtv, dl, dm, ALU.subtract))
            dve.wait_ge(steps.sem, k)
            nc.vector.tensor_tensor(heads(av), heads(dtv), nega[:].unsqueeze(1).to_broadcast([P, NC, NH]),
                                    ALU.mult).then_inc(dt_a.sem, 1)

        @block.vector
        def _(dve):
            steps = Steps(dve_steps, DVE_STEPS)
            dve.wait_ge(d_con, 32)
            steps.step(nc.vector.tensor_scalar(cmean[:], ones, 1.0 / E, None, ALU.mult))
            dve.wait_ge(d_x0, 16)
            dve_ln(dve, steps, 0)
            dve.wait_ge(alog_e, 1)
            steps.step(nc.vector.tensor_scalar(nega[:], nega[:], -1.0, None, ALU.mult))
            for k in range(KD):
                dve.wait_ge(d_win[k], 16)
                s = steps.step(nc.vector.tensor_reduce(out=mx[:, k:k + 1], in_=win_raw[:, k, :], axis=AX.X, op=ALU.max,
                                                       apply_absolute_value=True))

            def to_scale(n, first, count, prev, want):
                dve.wait_ge(steps.sem, prev)
                nc.vector.tensor_reduce(out=mx[:, 24 + n:25 + n], in_=mx[:, first:first + count], axis=AX.X,
                                        op=ALU.max).then_inc(max_part, 1)
                dve.wait_ge(max_all, n + 1)
                v, q = mx[:, 28 + n:29 + n], p2[:, n:n + 1]
                k = steps.step(nc.vector.tensor_scalar(q.bitcast(I32), v.bitcast(I32), 0x7F800000, None, ALU.bitwise_and))
                dve.wait_ge(steps.sem, k)
                k = steps.step(nc.vector.tensor_scalar(q, q, 2.0 ** -20, None, ALU.max))
                dve.wait_ge(steps.sem, k)
                k = steps.step(nc.vector.reciprocal(scl[:, n:n + 1], q))
                steps.step(nc.vector.tensor_scalar(inv[:, n:n + 1], q, 2.0 ** -want, None, ALU.mult))
                dve.wait_ge(steps.sem, k)
                k = steps.step(nc.vector.tensor_scalar(scl[:, n:n + 1], scl[:, n:n + 1], 2.0 ** want, None, ALU.mult))
                dve.wait_ge(steps.sem, k)

            dve_xl(dve, 0)
            to_scale(0, 0, KD, s, 14)
            steps.step(nc.vector.tensor_scalar(f_in[:], inv[:, 0:1], 1 / XS, None, ALU.mult))
            k = steps.step(nc.vector.tensor_scalar(f_half[:], inv[:, 0:1], 0.5 / XS, None, ALU.mult))
            dve.wait_ge(steps.sem, k)
            dve.wait_ge(d_par, 16 * N_PAR)
            steps.step(nc.vector.tensor_scalar(cw[:], cw[:], f_half[:, 0:1], None, ALU.mult))
            steps.step(nc.vector.tensor_scalar(cb[:], cb[:], 0.5, None, ALU.mult)) 
            nc.vector.tensor_scalar(p2[:, 3:4], p2[:, 0:1], 1.0, None, ALU.mult).then_inc(scale_ok, 1)
            dve.wait_ge(wdt_h, 1)
            nc.vector.scalar_tensor_tensor(out=wdt_lo[:], in0=win_raw[:, :, DT:DT + NH], scalar=scl[:, 0:1], in1=wdt_hi[:],
                                           op0=ALU.mult, op1=ALU.subtract).then_inc(wdt_h, 1)
            dve_dt(dve, steps, 0)
            dve.wait_ge(d_w2, 16)
            s = steps.step(nc.vector.tensor_reduce(out=mx[:, 4:5], in_=w2a, axis=AX.XY, op=ALU.max, apply_absolute_value=True))
            for n in range(4):
                butterfly(nc.vector, dve, n, 0, D_SPLIT, bf_dve, steps if n == 0 else None, s)
            dve.wait_ge(d_wo, 16)
            for q in range(QE):
                s = steps.step(nc.vector.tensor_scalar(wo_raw[:, q, :], wo_raw[:, q, :], nw[:, q:q + 1], None, ALU.mult))
            dve.wait_ge(steps.sem, s)
            s = steps.step(nc.vector.tensor_reduce(out=mx[:, 5:6], in_=wo_raw, axis=AX.XY, op=ALU.max, apply_absolute_value=True))
            for i in range(2 * KD):
                dve.wait_ge(d_w13[i % 4], 16 * (i // 4 + 1))
                nc.vector.tensor_reduce(out=mx[:, 8 + i:9 + i], in_=w13_raw[i % 4], axis=AX.X, op=ALU.max,
                                        apply_absolute_value=True).then_inc(w13_seen, 1)
            dve.wait_ge(w13_seen, 2 * KD)
            to_scale(1, 8, 2 * KD, s, 14)
            to_scale(2, 5, 1, s, 14)
            to_scale(3, 4, 1, s, 8)
            steps.step(nc.vector.tensor_scalar(f_13[:], inv[:, 1:2], 0.5 / XS, None, ALU.mult))
            steps.step(nc.vector.tensor_scalar(f_out[:], inv[:, 2:3], 1 / XS, None, ALU.mult))
            steps.step(nc.vector.tensor_scalar(f_had[:], scl[:, 3:4], float(np.float32(1 / np.sqrt(HF))), None, ALU.mult))
            k = steps.step(nc.vector.tensor_scalar(f_w2[:], inv[:, 1:2], inv[:, 1:2], 2.0 ** 33, ALU.mult, ALU.mult))
            dve.wait_ge(steps.sem, k)
            k = steps.step(nc.vector.tensor_tensor(f_w2[:], f_w2[:], inv[:, 3:4], ALU.mult))
            dve.wait_ge(steps.sem, k)
            nc.vector.tensor_copy(p2[:, 0:1], p2[:, 1:2]).then_inc(scale_ok, 2)
            for q in range(QE):
                dve.wait_ge(wo_h, q + 1)
                k = steps.step(nc.vector.scalar_tensor_tensor(out=wo_lo[:, q, :], in0=wo_raw[:, q, :], scalar=scl[:, 2:3],
                                                              in1=wo_hi[:, q, :], op0=ALU.mult, op1=ALU.subtract))
            for j in range(JF):
                dve.wait_ge(had_hi, j + 1)
                nc.vector.scalar_tensor_tensor(out=w2p[:, j, D:2 * D], in0=bank(j % 4), scalar=f_had[:, 0:1],
                                               in1=w2p[:, j, 0:D], op0=ALU.mult, op1=ALU.subtract).then_inc(had_lo, 1)
            dve.wait_ge(had_lo, JF)
            dve.wait_ge(steps.sem, k)
            dve.nop().then_inc(ready, 1)
            dve.wait_ge(ready, ENGINES_READY)
            def split_lo(b, p):
                dve.wait_ge(w_hi.sem, w_hi.at(b, p))
                nc.vector.scalar_tensor_tensor(out=part_lo[p % PARTS], in0=raw[p % RAW], scalar=weight_scale(STREAM[p % NT]),
                                               in1=part_hi[p % PARTS], op0=ALU.mult, op1=ALU.subtract).then_inc(w_lo.sem, 1)

            for p in range(AHEAD):
                split_lo(0, p)
            with dve.Fori(0, NB) as b:
                steps.enter(b)

                def finish(key):
                    kind, i = key
                    p = POS[key]
                    src = tile_bank(p)
                    if kind == "C":
                        n = C_ORDER[i]
                        a = acc[n % 2]
                        dve.wait_ge(acc_ok.sem, acc_ok.at(b, n))
                        for s in range(1, TAPS):
                            ins = nc.vector.scalar_tensor_tensor(out=a[:, s:L], in0=src[:, 0:L - s],
                                                                 scalar=cw[:, i, TAPS - 1 - s:TAPS - s], in1=a[:, s:L],
                                                                 op0=ALU.mult, op1=ALU.add)
                            if s < TAPS - 1:
                                dve.wait_ge(steps.sem, steps.step(ins))
                        ins.then_inc(evac.sem, 1)
                        dve.wait_ge(tanh_ok.sem, tanh_ok.at(b, TANH[key]))
                        nc.vector.scalar_tensor_tensor(out=XT[:, i, :], in0=tb[TANH[key] % 2], scalar=1.0, in1=a,
                                                       op0=ALU.add, op1=ALU.mult).then_inc(xt_done.sem, 1)
                    elif kind == "Z":
                        dve.wait_ge(tanh_ok.sem, tanh_ok.at(b, TANH[key]))
                        nc.vector.scalar_tensor_tensor(out=gz[:, i, :], in0=tb[TANH[key] % 2], scalar=1.0, in1=src,
                                                       op0=ALU.add, op1=ALU.mult).then_inc(evac.sem, 1)
                    elif kind == "A":
                        dve.wait_ge(tanh_ok.sem, tanh_ok.at(b, TANH[key]))
                        dve.wait_ge(hid_l.sem, hid_l.at(b, max(i - 2, -1)))
                        nc.vector.scalar_tensor_tensor(out=hs[i % 2], in0=tb[TANH[key] % 2], scalar=1.0, in1=src,
                                                       op0=ALU.add, op1=ALU.mult).then_inc(evac.sem, 1)
                    else:
                        dve.wait_ge(tile_done.sem, tile_done.at(b, p))
                        dve.wait_ge(evac.sem, evac.at(b, p - 1))
                        nc.vector.scalar_tensor_tensor(out=hs[i % 2], in0=src, scalar=2.0 ** -33 / (2 * XS * XS), in1=hs[i % 2],
                                                       op0=ALU.mult, op1=ALU.mult).then_inc(evac.sem, 1)

                k = steps.step(nc.vector.tensor_copy(rp1_cur, rp1))
                k = steps.step(nc.vector.tensor_copy(nmr_cur, nmr))
                for kind, i in SCHEDULE:
                    c = i
                    if kind in "CZAU":
                        split_lo(b, POS[kind, i] + AHEAD)
                        finish((kind, i))
                    elif kind == "T":
                        dve.wait_ge(pe_x.sem, pe_x.at(b, c))
                        nc.vector.tensor_tensor(Xdt.rearrange("p (h d) -> p h d", h=NH),
                                                bank(4, 2).rearrange("p (h d) -> p h d", h=NH),
                                                dtv[:, c * NH:(c + 1) * NH].unsqueeze(2).to_broadcast([P, NH, HD]),
                                                ALU.mult).then_inc(xdt_ok.sem, 1)
                        dve.wait_ge(pe_g.sem, pe_g.at(b, c))
                        nc.vector.tensor_tensor(Gm, bank(7)[:, 0:P], tri_le, ALU.mult).then_inc(gm_ok.sem, 1)
                    elif kind == "X":
                        dve.wait_ge(eexp_ok.sem, eexp_ok.at(b, c))
                        dve.wait_ge(gm_ok.sem, gm_ok.at(b, c))
                        nc.vector.tensor_tensor(Eb, Eb, Gm.unsqueeze(1).to_broadcast([P, NH, P]), ALU.mult).then_inc(m_ok.sem, 1)
                    elif kind == "S":
                        if c > 0:
                            dve.wait_ge(pe_off.sem, pe_off.at(b, c - 1))
                            dve.wait_ge(d_ecsb, (b * (NC - 1) + c) * 32)
                            nc.vector.tensor_tensor(t1, bank(6, 2), ecsb, ALU.mult).then_inc(t1_ok.sem, 1)
                    elif kind == "R":
                        if 0 < c < NC - 1:
                            dve.wait_ge(pe_state.sem, pe_state.at(b, c))
                            dve.wait_ge(sdec_ok.sem, sdec_ok.at(b, c - 1))
                            nc.vector.tensor_tensor(state, bank(4, 2), state, ALU.add).then_inc(state_ok.sem, 1)
                    elif kind == "Y":
                        dve.wait_ge(pe_diag.sem, pe_diag.at(b, c))
                        if c > 0:
                            dve.wait_ge(t2_ok.sem, t2_ok.at(b, c - 1))
                        else:
                            dve.wait_ge(xd_ok.sem, xd_ok.at(b, c))
                        nc.vector.tensor_tensor(y, bank(6, 2), XD, ALU.add).then_inc(diag_read.sem, 1)
                        dve.wait_ge(diag_read.sem, diag_read.at(b, c))
                        y3 = y.rearrange("p (q l) -> p q l", q=QE)
                        nc.vector.scalar_tensor_tensor(out=y3, in0=y3, scalar=f_half[:, 0:1], in1=gz[:, :, c * P:(c + 1) * P],
                                                       op0=ALU.mult, op1=ALU.mult).then_inc(ygate_ok.sem, 1)
                    elif kind == "Q":
                        dve.wait_ge(sq_ok.sem, sq_ok.at(b, c))
                        nc.vector.tensor_reduce(out=sqr, in_=t1.rearrange("p (q l) -> p l q", q=QE), axis=AX.X,
                                                op=ALU.add).then_inc(sqr_ok.sem, 1)
                    elif kind == "N":
                        dve.wait_ge(pe_mean.sem, pe_mean.at(b, c))
                        nc.vector.tensor_scalar(nv, out_bank(c)[0][:, 0:P], EPS, None, ALU.add).then_inc(mean_read.sem, 1)
                        dve.wait_ge(mean_read.sem, mean_read.at(b, c))
                        rsqrt(dve, steps, nv, nr, ntmp, sqr)
                        y3 = y.rearrange("p (q l) -> p q l", q=QE)
                        nc.vector.tensor_tensor(y3, y3, nr.unsqueeze(1).to_broadcast([P, QE, P]), ALU.mult).then_inc(yn_ok.sem, 1)
                    elif kind == "V":
                        y3 = y.rearrange("p (q l) -> p q l", q=QE)
                        dve.wait_ge(yh_ok.sem, yh_ok.at(b, c))
                        nc.vector.scalar_tensor_tensor(out=yl, in0=y3, scalar=XS, in1=yh, op0=ALU.mult,
                                                       op1=ALU.subtract).then_inc(yl_ok.sem, 1)
                    elif kind == "W":
                        dve.wait_ge(d_xr[c % 2], (b * (NC // 2) + (c // 2 + 1)) * 16)
                        k = steps.step(nc.vector.tensor_scalar(xr[c % 2], xr[c % 2], rp1_cur[:, c:c + 1], nmr_cur[:, c:c + 1],
                                                               ALU.mult, ALU.add))
                        dve.wait_ge(steps.sem, k)
                        dve.wait_ge(pe_wout.sem, pe_wout.at(b, c))
                        if c == 0:
                            dve.wait_ge(d_out, b * (NC * 16) + 1)
                        nc.vector.scalar_tensor_tensor(out=racc[:, c, :], in0=out_bank(c)[1], scalar=f_out[:, 0:1], in1=xr[c % 2],
                                                       op0=ALU.mult, op1=ALU.add).then_inc(mamba_evac.sem, 1)
                    elif kind == "LN":
                        dve.wait_ge(d_xraw, (b + 1) * 16)
                        dve_ln(dve, steps, b + 1)
                    elif kind == "XT":
                        dve_xl(dve, b + 1)
                    elif kind == "DT":
                        dve_dt(dve, steps, b + 1)
                    elif kind == "OUT":
                        dve.wait_ge(w2_used.sem, w2_used.at(b, JF - 1))
                        dve.wait_ge(mamba_evac.sem, mamba_evac.at(b, NC - 1))
                        for t in range(NC):
                            nc.vector.scalar_tensor_tensor(out=racc[:, t, :], in0=bank(t), scalar=f_w2[:, 0:1],
                                                           in1=racc[:, t, :], op0=ALU.mult, op1=ALU.add).then_inc(ffn_evac.sem, 1)
                steps.leave()

        @block.gpsimd
        def _(pool):
            def all_max(n):
                pool.wait_ge(max_part, n + 1)
                nc.gpsimd.partition_all_reduce(mx[:, 28 + n:29 + n], mx[:, 24 + n:25 + n], P,
                                               bass.bass_isa.ReduceOp.max).then_inc(max_all, 1)
            all_max(0)
            pool.wait_ge(d_w2, 16)
            for n in range(4):
                if n == 1:
                    pool.wait_ge(bf_dve, 1)
                butterfly(nc.gpsimd, pool, n, D_SPLIT, D, bf_pool, None, None)
            for n in range(1, 4):
                all_max(n)
            pool.nop().then_inc(ready, 1)
            pool.wait_ge(ready, ENGINES_READY)
            with pool.Fori(0, NB) as b:
                for kind, i in SCHEDULE:
                    c = i
                    if kind == "U":
                        pool.wait_ge(hid_h.sem, hid_h.at(b, i))
                        nc.gpsimd.tensor_tensor(hid_lo[:, i, :], hs[i % 2], hid_hi[:, i, :], ALU.subtract).then_inc(hid_l.sem, 1)
                    elif kind == "E":
                        pool.wait_ge(d_csbc, (b * NC + (c + 1)) * 16)
                        pool.wait_ge(sums_ok.sem, sums_ok.at(b, 0))
                        pool.wait_ge(pe_diag.sem, pe_diag.at(b, c - 1))
                        nc.gpsimd.tensor_tensor(Eb, csbc, cs_s[:, c * NH:(c + 1) * NH].unsqueeze(2).to_broadcast([P, NH, P]),
                                                ALU.subtract).then_inc(esub_ok.sem, 1)
                        pool.wait_ge(esub_ok.sem, esub_ok.at(b, c))
                        nc.gpsimd.tensor_tensor(pool_mark, ones[:, 0:1], ones[:, 0:1], ALU.mult)
                        nc.gpsimd.tensor_scalar(Eb, Eb, 0.0, -3.0e38, ALU.min, ALU.max).then_inc(emin_ok.sem, 1)
                    elif kind == "T":
                        if c < NC - 1:
                            pool.wait_ge(xdt_ok.sem, xdt_ok.at(b, c))
                            nc.gpsimd.tensor_tensor(Xdec.rearrange("p (h d) -> p h d", h=NH), Xdt.rearrange("p (h d) -> p h d", h=NH),
                                                    dec[:, c * NH:(c + 1) * NH].unsqueeze(2).to_broadcast([P, NH, HD]),
                                                    ALU.mult).then_inc(xdec_ok.sem, 1)
                    elif kind == "S" and c > 0:
                        pool.wait_ge(t1_ok.sem, t1_ok.at(b, c - 1))
                        pool.wait_ge(xd_ok.sem, xd_ok.at(b, c))
                        nc.gpsimd.tensor_tensor(XD, XD, t1, ALU.add).then_inc(t2_ok.sem, 1)
                        if c < NC - 1:
                            nc.gpsimd.tensor_tensor(state.rearrange("p (h d) -> p h d", h=NH), state.rearrange("p (h d) -> p h d", h=NH),
                                                    tot[:, c * NH:(c + 1) * NH].unsqueeze(2).to_broadcast([P, NH, HD]),
                                                    ALU.mult).then_inc(sdec_ok.sem, 1)


def constants():
    k = np.arange(P)
    bits = np.array([[bin(a & c).count("1") for c in k] for a in k])
    return np.concatenate([np.eye(P), k[:, None] <= k[None, :], k[:, None] > k[None, :],
                           np.ones((P, P)), 1.0 - 2.0 * (bits % 2)], axis=1).astype(np.float32)


def kernel(L0_attn_x, L0_attn_w_in, L0_attn_conv_w, L0_attn_conv_b, L0_attn_dt_bias, L0_attn_A_log, L0_attn_D,
           L0_attn_norm_w, L0_attn_w_out, L0_ffn_W1, L0_ffn_W2, L0_ffn_W3):
    import concourse.bacc as _bacc
    from concourse.bass_utils import run_bass_kernel_spmd as _run

    x = np.asarray(L0_attn_x)
    con = np.ascontiguousarray
    arrays = {
        "x": con(np.concatenate([x, x[:1]])),
        "w_in": con(L0_attn_w_in),
        "w1t": con(np.asarray(L0_ffn_W1).T),
        "w3t": con(np.asarray(L0_ffn_W3).T),
        "w2t": con(np.asarray(L0_ffn_W2).T),
        "w_out": con(L0_attn_w_out),
        "conv_w": con(np.asarray(L0_attn_conv_w).reshape(MC, P, TAPS).transpose(1, 0, 2)),
        "conv_b": con(np.asarray(L0_attn_conv_b).reshape(MC, P).T),
        "dt_bias": con(np.broadcast_to(np.asarray(L0_attn_dt_bias), (P, NH))),
        "a_log": con(np.broadcast_to(np.asarray(L0_attn_A_log), (P, NH))),
        "d_cols": con(np.repeat(np.asarray(L0_attn_D), HD).reshape(QE, P).T),
        "norm_w": con(np.asarray(L0_attn_norm_w).reshape(QE, P).T),
        "consts": constants(),
    }
    nc = _bacc.Bacc("TRN2", target_bir_lowering=False, num_devices=1)
    args = [nc.dram_tensor(n, a.shape, mybir.dt.from_np(a.dtype), kind="ExternalInput").ap() for n, a in arrays.items()]
    out = nc.dram_tensor("out", (NB, L, D), FP32, kind="ExternalOutput").ap()
    build(nc, *args, out)
    r = _run(nc, [arrays], core_ids=[0])
    return r.results[0]["out"]
```

```python
import numpy as np
import concourse.bass as bass
from concourse import mybir
from contextlib import ExitStack

FP32, FP16, BF16, I32 = mybir.dt.float32, mybir.dt.float16, mybir.dt.bfloat16, mybir.dt.int32
ALU, ACT, AX = mybir.AluOpType, mybir.ActivationFunctionType, mybir.AxisListType

P = 128
NB, L, D = 4, 512, 512
KD = D // P
E, NH, HD, NS = 1024, 16, 64, 128
QE = E // P
CONV = E + 2 * NS
MC, MZ = CONV // P, E // P
TAPS = 4
NC = L // P
HF = 2048
JF = HF // P
EPS = 1e-5
HID = 2.0 ** -24
XS = 1024.0
NT = MC + MZ + 2 * JF
RAW, PARTS, W2R = 2, 5, 4
AHEAD = 3
FREE_BANK = 3
DT = 2 * E + 2 * NS
B_TILE, C_TILE = QE, QE + 1

STEP_AT = {
    "T": (3, 7, 17, 26),
    "X": (3, 11, 18, 29),
    "S": (6, 12, 20, 27),
    "R": (8, 16, 24, 35),
    "E": (None, 6, 14, 22),
    "Y": (6, 14, 22, 32),
    "Q": (6, 16, 24, 34),
    "N": (9, 17, 26, 35),
    "V": (9, 17, 28, 36),
    "W": (12, 20, 31, 40),
}
PREP_AT = {"LN": 35, "XT": 40, "DT": 41, "SUM": 48}
FRONT = "CZCCZCZCZCZCPCZCZCPZ"


def make_schedule():
    tiles = [(k, j) for j in range(JF) for k in "AU"] + [("G", j) for j in range(JF)]
    convs, gates, pairs = [B_TILE, C_TILE] + list(range(QE)), list(range(MZ)), 0
    seq = []
    for f in FRONT:
        if f == "P":
            seq += tiles[2 * pairs:2 * pairs + 2]
            pairs += 1
        else:
            seq.append((f, (convs if f == "C" else gates).pop(0)))
        if seq[-1] == ("C", C_TILE):
            seq.append(("E", 0))
    steps = [(at, 0, (kind, 0)) for kind, at in PREP_AT.items()]
    steps += [(at, n, (kind, c)) for n, (kind, places) in enumerate(STEP_AT.items(), 1)
              for c, at in enumerate(places) if at is not None]
    n = 2 * pairs
    for at, _, item in sorted(steps):
        seq += tiles[n:at]
        n = max(n, at)
        seq.append(item)
    return seq + tiles[n:] + [("OUT", 0)]


SCHEDULE = make_schedule()
STREAM = [key for key in SCHEDULE if key[0] in "CZAU"]
POS = {key: n for n, key in enumerate(STREAM)}

TANH_KEYS = []
for n, key in enumerate(STREAM):
    TANH_KEYS += [key] * (key[0] in "ZA") + [STREAM[n - 1]] * (n > 0 and STREAM[n - 1][0] == "C")
TANH = {key: n for n, key in enumerate(TANH_KEYS)}
NTANH = len(TANH)
C_ORDER = {key[1]: n for n, key in enumerate(k for k in STREAM if k[0] == "C")}

DVE_STEPS, ACT_STEPS = 103, 1


class Signal:

    def __init__(self, sem, per_batch, start):
        self.sem, self.per_batch, self.start = sem, per_batch, start

    def at(self, nb, i):
        assert self.start + i >= 0
        return nb * self.per_batch + (self.start + i + 1)


class Steps:

    def __init__(self, sem, per_batch):
        self.sem, self.per_batch, self.n, self.base, self.b = sem, per_batch, 0, 0, 0

    def step(self, ins):
        ins.then_inc(self.sem, 1)
        self.n += 1
        return self.b * self.per_batch + (self.base + self.n)

    def enter(self, b):
        self.base, self.n, self.b = self.n, 0, b

    def leave(self):
        assert self.n == self.per_batch, self.n


def build(nc, x, w_in, w1t, w3t, w2t, w_out, conv_w, conv_b, dt_bias, a_log, d_cols, norm_w, consts, out):
    w2_parts = nc.dram_tensor("w2_parts", (JF, P, 2 * D), FP16, kind="Internal").ap()
    cs_rows = nc.dram_tensor("cs_rows", (NB + 1, NC, NH, P), FP32, kind="Internal").ap()
    ecs_rows = nc.dram_tensor("ecs_rows", (NB + 1, NC, NH, P), FP32, kind="Internal").ap()
    ctx = ExitStack()
    with ctx:
        def sb(name, shape, dt=FP32):
            return ctx.enter_context(nc.sbuf_tensor(name, shape, dt))

        def sem(name):
            return ctx.enter_context(nc.semaphore(name))

        con = sb("con", [P, 4 * P])
        ident, tri_le, tri_gt, ones = (con[:, i * P:(i + 1) * P] for i in range(4))
        cmean = sb("cmean", [P, P])
        wo_hi, wo_lo = sb("wo_hi", [P, QE, D], FP16), sb("wo_lo", [P, QE, D], FP16)
        xh, xl = sb("xh", [P, KD, L], FP16), sb("xl", [P, KD, L], FP16)
        wdt_hi, wdt_lo = sb("wdt_hi", [P, KD, NH], FP16), sb("wdt_lo", [P, KD, NH], FP16)
        cw, cb = sb("cw", [P, MC, TAPS]), sb("cb", [P, MC])
        dtb, nega, dcol, nw = sb("dtb", [P, NH]), sb("nega", [P, NH]), sb("dcol", [P, QE]), sb("nw", [P, QE])
        scl, inv, mx = sb("scl", [P, 4]), sb("inv", [P, 4]), sb("mx", [P, 32])
        p2 = sb("p2", [P, 4])
        row_sq, nws, total = mx[:, 0:16], mx[:, 16:24], mx[:, 24:28]
        pool_mark = mx[:, 31:32]
        f_in, f_half, f_13, f_out, f_w2, f_had = (sb(n, [P, 1]) for n in ("f_in", "f_half", "f_13", "f_out", "f_w2", "f_had"))

        arena_words = 46150
        STAGED = KD * (DT + NH) + 2 * JF * D + QE * D + P
        arena = sb("arena", [P, arena_words])
        used = [0]

        def view(words, dt=FP32):
            a = arena[:, used[0]:used[0] + words]
            used[0] += words
            return a if dt == FP32 else a.bitcast(dt)

        def cut(v, n):
            return v.rearrange("p (a b) -> p a b", a=n)

        hid_hi, hid_lo = cut(view(JF * L // 2, FP16), JF), cut(view(JF * L // 2, FP16), JF)
        XT = cut(view(MC * L), MC)
        gz = cut(view(MZ * L), MZ)
        csbc, Eb = cut(view(NH * P), NH), cut(view(NH * P), NH)
        Xdt, Xdec, ecsb, state, t1, XD, y = (view(E) for _ in range(7))
        Bs, Gm = view(P), view(P)
        sqr, nv, nr, ntmp = (view(P) for _ in range(4))
        yh, yl = cut(view(E // 2, FP16), QE), cut(view(E // 2, FP16), QE)
        assert used[0] >= STAGED
        raw = [cut(view(KD * P), KD) for _ in range(RAW)]
        part_hi = [cut(view(KD * P // 2, FP16), KD) for _ in range(PARTS)]
        part_lo = [cut(view(KD * P // 2, FP16), KD) for _ in range(PARTS)]
        tb, acc, hs = ([view(L) for _ in range(2)] for _ in range(3))
        w2s = [cut(view(D, FP16), 2) for _ in range(W2R)]
        xraw = cut(view(NC * D), NC)
        racc_at = used[0]
        racc = cut(view(NC * D), NC)
        xr = [view(D) for _ in range(2)]
        W4 = NC * NH
        dr, de, du, dl, dm, dtv, av, cs_s, dec, tot = (view(W4) for _ in range(10))
        csT, ecsT = view(L)[0:NH, :], view(L)[0:NH, :]
        st = cut(view(NC * 6), NC)
        mv = cut(view(NC * 2), NC)
        lv, lr, lt, lm = (view(NC) for _ in range(4))
        rstd, nmr, rp1, nmr_cur, rp1_cur = (view(NC) for _ in range(5))

        sq_act = [racc.rearrange("p a b -> p (a b)").bitcast(BF16)[:, i * HF:(i + 1) * HF] for i in range(2)]
        sq_pool = [xraw.rearrange("p a b -> p (a b)").bitcast(BF16)[:, i * HF:(i + 1) * HF] for i in range(2)]
        SQ_ROOM = (NC * D + 2 * D) // 2
        sq_place = [arena[:, racc_at + i * SQ_ROOM:racc_at + (i + 1) * SQ_ROOM].bitcast(BF16) for i in range(2)]
        ones16 = tb[0].bitcast(BF16)[:, 0:P]
        used_p = [0]

        def stage(words):
            a = arena[:, used_p[0]:used_p[0] + words]
            used_p[0] += words
            return a
        win_raw = cut(stage(KD * (DT + NH)), KD)
        w2a, w2b = cut(stage(JF * D), JF), cut(stage(JF * D), JF)
        wo_raw = cut(stage(QE * D), QE)
        hadam = stage(P)
        assert used_p[0] == STAGED
        assert 4 * HF <= KD * (DT + NH)
        w13_raw = [arena[:, i * HF:(i + 1) * HF] for i in range(4)]
        w2p = w2b.rearrange("p a b -> p (a b)").bitcast(FP16).rearrange("p (a c) -> p a c", a=JF)

        ps = ctx.enter_context(nc.psum_tensor("ps", [P, 8 * L], FP32))

        def bank(i, n=1):
            return ps[:, i * L:(i + n) * L]

        d_con, d_par, d_x0 = sem("d_con"), sem("d_par"), sem("d_x0")
        d_win = [sem(f"d_win{k}") for k in range(KD)]
        d_wo, d_w2 = sem("d_wo"), sem("d_w2")
        d_w13 = [sem(f"d_w13_{k}") for k in range(4)]
        d_w2st = sem("d_w2st")
        d_raw = [sem(f"d_raw{i}") for i in range(RAW)]
        d_w2s = [sem(f"d_w2s{i}") for i in range(W2R)]
        d_xraw, d_cst, d_csbc, d_ecsb, d_out = sem("d_xraw"), sem("d_cst"), sem("d_csbc"), sem("d_ecsb"), sem("d_out")
        d_xr = [sem(f"d_xr{i}") for i in range(2)]
        sq_ok_w, sums_w, scale_ok = sem("sq_ok_w"), sem("sums_w"), sem("scale_ok")
        w13_sq_act, w13_sq_pool, w13_sums = sem("w13_sq_act"), sem("w13_sq_pool"), sem("w13_sums")
        ones16_ok, w13_read, w13_scale = sem("ones16_ok"), sem("w13_read"), sem("w13_scale")
        wdt_h, wo_h, alog_e = sem("wdt_h"), sem("wo_h"), sem("alog_e")
        bf_dve, bf_pool, had_done, had_hi, had_lo = sem("bf_dve"), sem("bf_pool"), sem("had_done"), sem("had_hi"), sem("had_lo")
        ready = sem("ready")
        signals = []

        def signal(name, per_batch, start=0):
            signals.append(Signal(sem(name), per_batch, start))
            return signals[-1]

        w_hi = signal("w_hi", NT)
        w_lo = signal("w_lo", NT, RAW)
        tile_done = signal("tile_done", NT, PARTS)
        evac = signal("evac", NT, 1)
        acc_ok = signal("acc_ok", MC)
        tanh_ok = signal("tanh_ok", NTANH)
        xt_done = signal("xt_done", MC, 1)
        hid_h = signal("hid_h", JF)
        hid_l = signal("hid_l", JF, 1)
        w2_used = signal("w2_used", JF, W2R)
        ffn_evac = signal("ffn_evac", NC, NC)
        pe_x = signal("pe_x", NC)
        pe_b = signal("pe_b", NC)
        pe_g = signal("pe_g", NC)
        pe_off = signal("pe_off", NC - 1)
        pe_state = signal("pe_state", NC - 1)
        pe_diag = signal("pe_diag", NC, 1)
        pe_mean = signal("pe_mean", NC)
        pe_wout = signal("pe_wout", NC, 1)
        gm_ok = signal("gm_ok", NC)
        xdt_ok = signal("xdt_ok", NC)
        bs_ok = signal("bs_ok", NC)
        xd_ok = signal("xd_ok", NC)
        xdec_ok = signal("xdec_ok", NC - 1)
        esub_ok = signal("esub_ok", NC, 1)
        emin_ok = signal("emin_ok", NC)
        eexp_ok = signal("eexp_ok", NC)
        m_ok = signal("m_ok", NC)
        t1_ok = signal("t1_ok", NC - 1, 1)
        t2_ok = signal("t2_ok", NC - 1)
        state0_ok = signal("state0_ok", 1)
        sdec_ok = signal("sdec_ok", NC - 2)
        state_ok = signal("state_ok", NC - 2)
        diag_read = signal("diag_read", NC, 1)
        ygate_ok = signal("ygate_ok", NC)
        sq_ok = signal("sq_ok", NC)
        sqr_ok = signal("sqr_ok", NC)
        mean_read = signal("mean_read", NC)
        yn_ok = signal("yn_ok", NC)
        yh_ok = signal("yh_ok", NC)
        yl_ok = signal("yl_ok", NC)
        mamba_evac = signal("mamba_evac", NC, 1)
        ln_ok = signal("ln_ok", 1)
        xn_ok = signal("xn_ok", NC)
        pe_xt = signal("pe_xt", NC)
        xh_ok = signal("xh_ok", NC)
        xl_ok = signal("xl_ok", NC)
        pe_dt = signal("pe_dt", 1)
        dt_raw = signal("dt_raw", 1)
        dt_exp = signal("dt_exp", 1)
        dt_u = signal("dt_u", 1)
        dt_ln = signal("dt_ln", 1)
        dt_a = signal("dt_a", 1)
        pe_sums = signal("pe_sums", 1)
        pe_cst = signal("pe_cst", 1)
        sums_ok = signal("sums_ok", 1)
        cst_ok = signal("cst_ok", 1)
        ecst_ok = signal("ecst_ok", 1)
        dve_steps, act_steps = sem("dve_steps"), sem("act_steps")
        ENGINES_READY = 4
        N_PAR = 6

        def weight_tile(key):
            kind, i = key
            if kind == "C":
                src, col = w_in, E + i * P
            elif kind == "Z":
                src, col = w_in, i * P
            elif kind == "A":
                src, col = w1t, i * P
            else:
                src, col = w3t, i * P
            return src.rearrange("(k p) n -> p k n", p=P)[:, :, col:col + P]

        def weight_scale(key):
            return scl[:, 0:1] if key[0] in "CZ" else scl[:, 1:2]

        def tile_bank(p):
            return bank(4 + p if p < 2 else (p - 2) % 3)

        def out_bank(c):
            return (bank(FREE_BANK), bank(FREE_BANK)) if c < NC - 1 else (bank(4), bank(5))

        block = ctx.enter_context(nc.Block())

        SQ_W2, SQ_IN, SQ_WO = KD, 2 * KD, 2 * KD + QE
        D_SPLIT = 320

        def butterfly(eng, e, n, lo, hi, done):
            h = 1 << n
            src, dst = (w2a, w2b) if n % 2 == 0 else (w2b, w2a)
            if n > 0:
                e.wait_ge(done, n)
            if n == 1:
                e.wait_ge(sq_ok_w, SQ_W2)
            v = src[:, :, lo:hi].rearrange("p (g two h) d -> p g two h d", two=2, h=h)
            w = dst[:, :, lo:hi].rearrange("p (g two h) d -> p g two h d", two=2, h=h)
            for g in range(JF // (2 * h)):
                eng.tensor_tensor(w[:, g, 0], v[:, g, 0], v[:, g, 1], ALU.add)
                last = eng.tensor_tensor(w[:, g, 1], v[:, g, 0], v[:, g, 1], ALU.subtract)
            last.then_inc(done, 1)

        def load_tile(sp, b, p):
            sp.wait_ge(w_lo.sem, w_lo.at(b, p - RAW))
            sp.dma_start(raw[p % RAW], weight_tile(STREAM[p % NT])).then_inc(d_raw[p % RAW], 16)

        def load_w2(sp, b, j):
            sp.wait_ge(w2_used.sem, w2_used.at(b, j - W2R))
            sp.dma_start(w2s[j % W2R], w2_parts[j].rearrange("p (a d) -> p a d", a=2)).then_inc(d_w2s[j % W2R], 16)

        @block.sync
        def _(sp):
            for s in signals:
                if s.start:
                    sp.sem_inc(s.sem, s.start)
            sp.sem_inc(d_out, 1)
            sp.dma_start(con[:], consts[:, 0:4 * P]).then_inc(d_con, 16)
            sp.dma_start(hadam, consts[:, 4 * P:5 * P]).then_inc(d_con, 16)
            for dst, src in ((cw, conv_w), (cb, conv_b), (dtb, dt_bias), (nega, a_log), (dcol, d_cols), (nw, norm_w)):
                sp.dma_start(dst[:], src).then_inc(d_par, 16)
            sp.dma_start(xraw, x[0].rearrange("(t p) d -> p t d", p=P)).then_inc(d_x0, 16)
            sp.dma_start(w2a, w2t.rearrange("(j p) d -> p j d", p=P)).then_inc(d_w2, 16)
            win_v = w_in.rearrange("(k p) n -> p k n", p=P)
            for k in range(KD):
                sp.dma_start(win_raw[:, k, :], win_v[:, k, :]).then_inc(d_win[k], 16)
            sp.dma_start(wo_raw, w_out.rearrange("(q p) d -> p q d", p=P)).then_inc(d_wo, 16)
            sp.wait_ge(wdt_h, 2)
            for i in range(2 * KD):
                src = (w1t, w3t)[i % 2].rearrange("(k p) n -> p k n", p=P)[:, i // 2, :]
                if i >= 4:
                    sp.wait_ge(w13_sq_pool if i % 2 else w13_sq_act, (i - 4) // 2 + 1)
                sp.dma_start(w13_raw[i % 4], src).then_inc(d_w13[i % 4], 16)
            for p in range(RAW):
                load_tile(sp, 0, p)
            for j in range(JF):
                sp.wait_ge(had_lo, j + 1)
                sp.dma_start(w2_parts[j], w2p[:, j, :]).then_inc(d_w2st, 16)
            for p in range(RAW, AHEAD):
                load_tile(sp, 0, p)
            with sp.Fori(0, NB) as b:
                for kind, i in SCHEDULE:
                    if kind in "CZAU":
                        load_tile(sp, b, POS[kind, i] + AHEAD)
                    if kind == "A" and i == 4:
                        sp.wait_ge(pe_xt.sem, pe_xt.at(b, NC - 1))
                        sp.dma_start(xraw, x[b + 1].rearrange("(t p) d -> p t d", p=P)).then_inc(d_xraw, 16)
                    if kind == "U" and i == JF - W2R:
                        sp.wait_ge(d_w2st, 16 * JF)
                    if kind == "U" and i >= JF - W2R:
                        load_w2(sp, b, i - (JF - W2R))
                    if kind == "G" and i < JF - W2R:
                        load_w2(sp, b, i + W2R)
                    if kind == "OUT":
                        for t in range(NC):
                            sp.wait_ge(ffn_evac.sem, ffn_evac.at(b, t))
                            sp.dma_start(out[b, t * P:(t + 1) * P, :], racc[:, t, :]).then_inc(d_out, 16)
            for i in range(RAW):
                sp.wait_ge(d_raw[i], (NB * (NT // RAW) + 1) * 16)
            sp.wait_ge(d_out, NB * NC * 16 + 1)

        def three(out_ap, lhs, rhs, n):
            for i in range(n):
                for s, (a, c) in enumerate(((0, 0), (0, 1), (1, 0))):
                    ins = nc.tensor.matmul(out_ap, lhs(i, a), rhs(i, c), start=(i == 0 and s == 0),
                                           stop=(i == n - 1 and s == 2))
            return ins

        def pe_transposes(pe, nb):
            for t in range(NC):
                pe.wait_ge(xn_ok.sem, xn_ok.at(nb, t))
                if t >= 2:
                    pe.wait_ge(xl_ok.sem, xl_ok.at(nb, t - 2))
                for k in range(KD):
                    ins = nc.tensor.transpose(bank(6 + t % 2)[:, k * P:(k + 1) * P], xraw[:, t, k * P:(k + 1) * P], ident)
                ins.then_inc(pe_xt.sem, 1)

        def pe_dt_proj(pe, nb):
            pe.wait_ge(xl_ok.sem, xl_ok.at(nb, NC - 1))
            xs, ws = (xh, xl), (wdt_hi, wdt_lo)
            for t in range(NC):
                ins = three(bank(6)[:, t * NH:(t + 1) * NH], lambda k, a: xs[a][:, k, t * P:(t + 1) * P],
                            lambda k, c: ws[c][:, k, :], KD)
            ins.then_inc(pe_dt.sem, 1)

        def pe_cumsums(pe, nb):
            pe.wait_ge(dt_a.sem, dt_a.at(nb, 0))
            nc.tensor.matmul(bank(7)[:, 0:W4], tri_le, av, start=True, stop=True)
            nc.tensor.matmul(bank(7)[:, W4:2 * W4], tri_gt, av, start=True, stop=True)
            nc.tensor.matmul(bank(7)[:, 2 * W4:3 * W4], ones, av, start=True, stop=True).then_inc(pe_sums.sem, 1)
            for t in range(NC):
                ins = nc.tensor.matmul(bank(6)[0:NH, t * P:(t + 1) * P], av[:, t * NH:(t + 1) * NH], tri_le,
                                       start=True, stop=True)
            ins.then_inc(pe_cst.sem, 1)

        @block.tensor
        def _(pe):
            pe.wait_ge(d_con, 32)
            pe_transposes(pe, 0)
            pe.wait_ge(sq_ok_w, SQ_IN)
            nc.tensor.matmul(bank(3)[:, 0:KD], ones, row_sq[:, SQ_W2:SQ_IN], start=True, stop=True).then_inc(sums_w, 1)
            pe.wait_ge(wdt_h, 2)
            pe_dt_proj(pe, 0)
            pe.wait_ge(sq_ok_w, SQ_WO)
            nc.tensor.matmul(bank(2)[:, 0:KD], ones, row_sq[:, 0:SQ_W2], start=True, stop=True)
            nc.tensor.matmul(bank(2)[:, KD:KD + QE], ones, row_sq[:, SQ_IN:SQ_WO], start=True, stop=True).then_inc(sums_w, 1)
            pe_cumsums(pe, 0)

            def column_sums(i):
                for squares, done in ((sq_act, w13_sq_act), (sq_pool, w13_sq_pool)):
                    pe.wait_ge(done, i + 1)
                    for n in range(HF // L):
                        ins = nc.tensor.matmul(bank(4 + n), ones16, squares[i % 2][:, n * L:(n + 1) * L],
                                               start=(i == 0 and squares is sq_act),
                                               stop=(i == KD - 1 and squares is sq_pool), skip_group_check=True)
                ins.then_inc(w13_sums, 1)

            pe.wait_ge(ecst_ok.sem, ecst_ok.at(0, 0))
            pe.wait_ge(ones16_ok, 1)
            pe.wait_ge(bf_dve, 4)
            pe.wait_ge(bf_pool, 4)
            pe.wait_ge(scale_ok, 3)
            for j in range(JF):
                if j >= 4:
                    pe.wait_ge(had_lo, j - 4 + 1)
                nc.tensor.matmul(bank(j % 4), hadam, w2a[:, j, :], start=True, stop=True).then_inc(had_done, 1)
                if j % 4 == 3:
                    column_sums(j // 4)
            pe.wait_ge(had_lo, JF)
            pe.wait_ge(w13_read, 1)
            pe.nop().then_inc(ready, 1)
            pe.wait_ge(ready, ENGINES_READY)
            xs, wos = (xh, xl), (wo_hi, wo_lo)
            with pe.Fori(0, NB) as b:
                def project(key):
                    p = POS[key]
                    pe.wait_ge(w_lo.sem, w_lo.at(b, p))
                    if p >= 5:
                        pe.wait_ge(evac.sem, evac.at(b, p - 3))
                    elif p >= 2:
                        pe.wait_ge(ffn_evac.sem, ffn_evac.at(b, p - 2 - NC))
                    w = (part_hi[p % PARTS], part_lo[p % PARTS])
                    three(tile_bank(p), lambda k, a: w[a][:, k, :], lambda k, c: xs[c][:, k, :], KD).then_inc(tile_done.sem, 1)

                for kind, i in SCHEDULE:
                    c = i
                    cols = slice(c * P, (c + 1) * P) if kind in "TXSYNW" else None
                    if kind in "CZAU":
                        project((kind, i))
                    elif kind == "T":
                        pe.wait_ge(xt_done.sem, xt_done.at(b, MC - 1))
                        if c == 0:
                            pe.wait_ge(d_w2st, 16 * JF)
                            pe.wait_ge(evac.sem, evac.at(b, 1))
                            pe.wait_ge(ecst_ok.sem, ecst_ok.at(b, 0))
                        else:
                            if c == 1:
                                pe.wait_ge(state0_ok.sem, state0_ok.at(b, 0))
                            else:
                                pe.wait_ge(state_ok.sem, state_ok.at(b, c - 2))
                            pe.wait_ge(diag_read.sem, diag_read.at(b, c - 1))
                        for q in range(QE):
                            ins = nc.tensor.transpose(bank(4, 2)[:, q * P:(q + 1) * P], XT[:, q, cols], ident)
                        ins.then_inc(pe_x.sem, 1)
                        nc.tensor.transpose(bank(6)[:, 0:P], XT[:, B_TILE, cols], ident).then_inc(pe_b.sem, 1)
                        nc.tensor.matmul(bank(7)[:, 0:P], XT[:, B_TILE, cols], XT[:, C_TILE, cols],
                                         start=True, stop=True).then_inc(pe_g.sem, 1)
                    elif kind == "S":
                        pe.wait_ge(bs_ok.sem, bs_ok.at(b, c))
                        pe.wait_ge(gm_ok.sem, gm_ok.at(b, c))
                        if c > 0:
                            if c == 1:
                                pe.wait_ge(state0_ok.sem, state0_ok.at(b, 0))
                            else:
                                pe.wait_ge(state_ok.sem, state_ok.at(b, c - 2))
                            for q in range(QE):
                                ins = nc.tensor.matmul(bank(6, 2)[:, q * P:(q + 1) * P], state[:, q * P:(q + 1) * P],
                                                       XT[:, C_TILE, cols], start=True, stop=True)
                            ins.then_inc(pe_off.sem, 1)
                        if c < NC - 1:
                            pe.wait_ge(xdec_ok.sem, xdec_ok.at(b, c))
                            for h in range(2):
                                ins = nc.tensor.matmul(bank(4 + h), Bs, Xdec[:, h * L:(h + 1) * L], start=True, stop=True)
                            ins.then_inc(pe_state.sem, 1)
                    elif kind == "Y":
                        pe.wait_ge(m_ok.sem, m_ok.at(b, c))
                        if c > 0:
                            pe.wait_ge(t1_ok.sem, t1_ok.at(b, c - 1))
                        for h in range(NH):
                            r, q = HD * (h % 2), h // 2
                            ins = nc.tensor.matmul(bank(6, 2)[r:r + HD, q * P:(q + 1) * P], Xdt[:, h * HD:(h + 1) * HD],
                                                   Eb[:, h, :], start=True, stop=True)
                        ins.then_inc(pe_diag.sem, 1)
                    elif kind == "N":
                        pe.wait_ge(sqr_ok.sem, sqr_ok.at(b, c))
                        if c == 0:
                            pe.wait_ge(ffn_evac.sem, ffn_evac.at(b, FREE_BANK - NC))
                        else:
                            pe.wait_ge(mamba_evac.sem, mamba_evac.at(b, c - 1))
                        nc.tensor.matmul(out_bank(c)[0][:, 0:P], cmean[:], sqr, start=True, stop=True).then_inc(pe_mean.sem, 1)
                    elif kind == "W":
                        pe.wait_ge(yl_ok.sem, yl_ok.at(b, c))
                        ys = (yh, yl)
                        three(out_bank(c)[1], lambda q, a: ys[a][:, q, :], lambda q, d: wos[d][:, q, :], QE).then_inc(pe_wout.sem, 1)
                    elif kind == "G":
                        pe.wait_ge(hid_l.sem, hid_l.at(b, i))
                        pe.wait_ge(d_w2s[i % W2R], (b * (JF // W2R) + (i // W2R + 1)) * 16)
                        hw = (hid_hi, hid_lo)
                        for t in (0, FREE_BANK, 1, 2):
                            if i == 0 and t == FREE_BANK:
                                pe.wait_ge(mamba_evac.sem, mamba_evac.at(b, NC - 2))
                            elif i == 0:
                                pe.wait_ge(evac.sem, evac.at(b, NT - 3 + t))
                            for s, (a, d) in enumerate(((0, 0), (0, 1), (1, 0))):
                                ins = nc.tensor.matmul(bank(t), hw[a][:, i, t * P:(t + 1) * P], w2s[i % W2R][:, d, :],
                                                       start=(i == 0 and s == 0), stop=(i == JF - 1 and s == 2),
                                                       skip_group_check=True)
                        ins.then_inc(w2_used.sem, 1)
                    elif kind == "XT":
                        pe.wait_ge(diag_read.sem, diag_read.at(b, NC - 1))
                        pe_transposes(pe, b + 1)
                    elif kind == "DT":
                        pe_dt_proj(pe, b + 1)
                    elif kind == "SUM":
                        pe_cumsums(pe, b + 1)

        def act_xn(act, nb):
            act.wait_ge(ln_ok.sem, ln_ok.at(nb, 0))
            for t in range(NC):
                nc.scalar.activation(xraw[:, t, :], xraw[:, t, :], ACT.Identity, bias=nmr[:, t:t + 1],
                                     scale=rstd[:, t:t + 1]).then_inc(xn_ok.sem, 1)

        def act_xh(act, nb):
            for t in range(NC):
                act.wait_ge(pe_xt.sem, pe_xt.at(nb, t))
                nc.scalar.activation(xh[:, :, t * P:(t + 1) * P], bank(6 + t % 2).rearrange("p (k n) -> p k n", k=KD),
                                     ACT.Copy, scale=XS).then_inc(xh_ok.sem, 1)

        def act_dt(act, steps, nb):
            act.wait_ge(dt_raw.sem, dt_raw.at(nb, 0))
            k = steps.step(nc.scalar.activation(de, dr, ACT.Abs))
            act.wait_ge(steps.sem, k)
            nc.scalar.activation(de, de, ACT.Exp, scale=-1.0).then_inc(dt_exp.sem, 1)
            act.wait_ge(dt_u.sem, dt_u.at(nb, 0))
            nc.scalar.activation(dl, du, ACT.Ln).then_inc(dt_ln.sem, 1)

        def act_sums(act, steps, nb):
            act.wait_ge(pe_sums.sem, pe_sums.at(nb, 0))
            nc.scalar.activation(cs_s, bank(7)[:, 0:W4], ACT.Copy)
            nc.scalar.activation(dec, bank(7)[:, W4:2 * W4], ACT.Exp)
            nc.scalar.activation(tot, bank(7)[:, 2 * W4:3 * W4], ACT.Exp).then_inc(sums_ok.sem, 1)
            act.wait_ge(pe_cst.sem, pe_cst.at(nb, 0))
            if not isinstance(nb, int):
                act.wait_ge(d_cst, nb * 32)
            nc.scalar.activation(csT, bank(6)[0:NH, :], ACT.Copy).then_inc(cst_ok.sem, 1)
            nc.scalar.activation(ecsT, bank(6)[0:NH, :], ACT.Exp).then_inc(ecst_ok.sem, 1)
            act.wait_ge(cst_ok.sem, cst_ok.at(nb, 0))
            act.dma_start(cs_rows[nb].rearrange("c h l -> h c l"), csT.rearrange("h (c l) -> h c l", c=NC)).then_inc(d_cst, 16)
            act.wait_ge(ecst_ok.sem, ecst_ok.at(nb, 0))
            act.dma_start(ecs_rows[nb].rearrange("c h l -> h c l"), ecsT.rearrange("h (c l) -> h c l", c=NC)).then_inc(d_cst, 16)

        @block.scalar
        def _(act):
            steps = Steps(act_steps, ACT_STEPS)
            act.wait_ge(d_par, 16 * N_PAR)
            nc.scalar.activation(nega[:], nega[:], ACT.Exp).then_inc(alog_e, 1)
            act_xn(act, 0)
            act_xh(act, 0)

            def square(n, w, scale=1.0):
                if n >= 2:
                    act.wait_ge(sq_ok_w, n - 1)
                words = int(np.prod(w.shape[1:]))
                assert words <= 2 * SQ_ROOM
                nc.scalar.activation(sq_place[n % 2][:, 0:words], w, ACT.Square, scale=scale,
                                     accum_out=row_sq[:, n:n + 1]).then_inc(sq_ok_w, 1)

            act.wait_ge(d_w2, 16)
            for k in range(KD):
                square(k, w2a.rearrange("p a b -> p (a b)")[:, k * HF:(k + 1) * HF])
            for k in range(KD):
                act.wait_ge(d_win[k], 16)
                square(SQ_W2 + k, win_raw[:, k, :])
            act.wait_ge(scale_ok, 1)
            nc.scalar.activation(wdt_hi[:], win_raw[:, :, DT:DT + NH], ACT.Copy, scale=scl[:, 0:1]).then_inc(wdt_h, 1)
            act.wait_ge(d_wo, 16)
            for q in range(QE):
                square(SQ_IN + q, wo_raw[:, q, :], nw[:, q:q + 1])
            act_dt(act, steps, 0)
            act_sums(act, steps, 0)
            act.wait_ge(sq_ok_w, SQ_WO)

            def square_w1(k):
                act.wait_ge(d_w13[2 * k % 4], 16 * (2 * k // 4 + 1))
                if k >= 2:
                    act.wait_ge(w13_sums, k - 1)
                nc.scalar.activation(sq_act[k % 2], w13_raw[2 * k % 4], ACT.Square).then_inc(w13_sq_act, 1)
            square_w1(0)
            square_w1(1)
            act.wait_ge(scale_ok, 3)
            for q in range(QE):
                nc.scalar.activation(wo_hi[:, q, :], wo_raw[:, q, :], ACT.Copy, scale=nws[:, q:q + 1]).then_inc(wo_h, 1)
            for j in range(JF):
                act.wait_ge(had_done, j + 1)
                nc.scalar.activation(w2p[:, j, 0:D], bank(j % 4), ACT.Copy, scale=f_had[:, 0:1]).then_inc(had_hi, 1)
                if j in (7, 11):
                    square_w1(j // 4 + 1)
            act.wait_ge(had_hi, JF)

            def split_hi(b, p):
                act.wait_ge(d_raw[p % RAW], (b * (NT // RAW) + (p // RAW + 1)) * 16)
                act.wait_ge(tile_done.sem, tile_done.at(b, p - PARTS))
                nc.scalar.activation(part_hi[p % PARTS], raw[p % RAW], ACT.Copy,
                                     scale=weight_scale(STREAM[p % NT])).then_inc(w_hi.sem, 1)

            for p in range(AHEAD):
                split_hi(0, p)
            act.nop().then_inc(ready, 1)
            act.wait_ge(ready, ENGINES_READY)
            act.wait_ge(w13_scale, 1)
            with act.Fori(0, NB) as b:
                steps.enter(b)

                def tanh_slot(key):
                    n = TANH[key]
                    if n < 2:
                        act.wait_ge(evac.sem, evac.at(b, -1))
                        return tb[n % 2]
                    kind, i = TANH_KEYS[n - 2]
                    if kind == "C":
                        act.wait_ge(xt_done.sem, xt_done.at(b, C_ORDER[i]))
                    else:
                        act.wait_ge(evac.sem, evac.at(b, POS[kind, i]))
                    return tb[n % 2]

                def finish(key):
                    kind, i = key
                    p = POS[key]
                    src = tile_bank(p)
                    if kind == "C":
                        n = C_ORDER[i]
                        act.wait_ge(tile_done.sem, tile_done.at(b, p))
                        act.wait_ge(xt_done.sem, xt_done.at(b, max(n - 2, -1)))
                        nc.scalar.activation(acc[n % 2], src, ACT.Identity, scale=cw[:, i, TAPS - 1:TAPS],
                                             bias=cb[:, i:i + 1]).then_inc(acc_ok.sem, 1)
                    elif kind in "ZA":
                        slot = tanh_slot(key)
                        act.wait_ge(tile_done.sem, tile_done.at(b, p))
                        nc.scalar.activation(slot, src, ACT.Tanh, scale=(f_half if kind == "Z" else f_13)[:, 0:1]).then_inc(tanh_ok.sem, 1)
                    else:
                        if i == 0:
                            act.wait_ge(w2_used.sem, w2_used.at(b, -1))
                        act.wait_ge(evac.sem, evac.at(b, p))
                        nc.scalar.activation(hid_hi[:, i, :], hs[i % 2], ACT.Copy).then_inc(hid_h.sem, 1)
                    if p > 0 and STREAM[p - 1][0] == "C":
                        last = STREAM[p - 1]
                        slot = tanh_slot(last)
                        act.wait_ge(evac.sem, evac.at(b, p - 1))
                        nc.scalar.activation(slot, acc[C_ORDER[last[1]] % 2], ACT.Tanh).then_inc(tanh_ok.sem, 1)

                for kind, i in SCHEDULE:
                    c = i
                    if kind in "CZAU":
                        split_hi(b, POS[kind, i] + AHEAD)
                        finish((kind, i))
                    elif kind == "E":
                        if c == 0:
                            act.wait_ge(d_w2st, 16 * JF)
                        act.wait_ge(d_cst, (b + 1) * 32)
                        act.wait_ge(esub_ok.sem, esub_ok.at(b, c - 1))
                        act.dma_start(csbc.rearrange("p h l -> p (h l)"),
                                      cs_rows[b, c].rearrange("h l -> (h l)").partition_broadcast(P)).then_inc(d_csbc, 16)
                        if c > 0:
                            act.wait_ge(t1_ok.sem, t1_ok.at(b, c - 2))
                            for r in range(2):
                                act.dma_start(ecsb[HD * r:HD * r + HD, :].rearrange("p (q l) -> p q l", q=QE),
                                              ecs_rows[b, c].rearrange("(q r) l -> r q l", r=2)[r].partition_broadcast(HD)).then_inc(d_ecsb, 16)
                    elif kind == "T":
                        act.wait_ge(mamba_evac.sem, mamba_evac.at(b, max(c - 2, -1)))
                        act.dma_start(xr[c % 2], x[b, c * P:(c + 1) * P, :]).then_inc(d_xr[c % 2], 16)
                        act.wait_ge(pe_b.sem, pe_b.at(b, c))
                        nc.scalar.activation(Bs, bank(6)[:, 0:P], ACT.Copy).then_inc(bs_ok.sem, 1)
                        act.wait_ge(diag_read.sem, diag_read.at(b, c - 1))
                        for q in range(QE):
                            ins = nc.scalar.activation(XD[:, q * P:(q + 1) * P], XT[:, q, c * P:(c + 1) * P], ACT.Copy,
                                                       scale=dcol[:, q:q + 1])
                        ins.then_inc(xd_ok.sem, 1)
                    elif kind == "X":
                        act.wait_ge(emin_ok.sem, emin_ok.at(b, c))
                        nc.scalar.activation(Eb, Eb, ACT.Exp).then_inc(eexp_ok.sem, 1)
                    elif kind == "S":
                        if c == 0:
                            act.wait_ge(pe_state.sem, pe_state.at(b, 0))
                            nc.scalar.activation(state, bank(4, 2), ACT.Copy).then_inc(state0_ok.sem, 1)
                    elif kind == "Y":
                        act.wait_ge(ygate_ok.sem, ygate_ok.at(b, c))
                        nc.scalar.activation(t1, y, ACT.Square).then_inc(sq_ok.sem, 1)
                    elif kind == "N":
                        act.wait_ge(yn_ok.sem, yn_ok.at(b, c))
                        act.wait_ge(pe_wout.sem, pe_wout.at(b, c - 1))
                        nc.scalar.activation(yh, y.rearrange("p (q l) -> p q l", q=QE), ACT.Copy, scale=XS).then_inc(yh_ok.sem, 1)
                    elif kind == "LN":
                        act_xn(act, b + 1)
                    elif kind == "XT":
                        act_xh(act, b + 1)
                    elif kind == "DT":
                        act_dt(act, steps, b + 1)
                    elif kind == "SUM":
                        act_sums(act, steps, b + 1)
                steps.leave()
            act.wait_ge(d_cst, (NB + 1) * 32)

        def rsqrt(dve, steps, v, r, tmp, vh):
            k = steps.step(nc.vector.tensor_scalar(tmp.bitcast(I32), v.bitcast(I32), 1, None, ALU.logical_shift_right))
            steps.step(nc.vector.tensor_scalar(vh, v, -0.5, None, ALU.mult))
            dve.wait_ge(steps.sem, k)
            k = steps.step(nc.vector.tensor_scalar(r.bitcast(I32), tmp.bitcast(I32), -1, 0x5F3759DF, ALU.mult, ALU.add))
            for _ in range(3):
                dve.wait_ge(steps.sem, k)
                k = steps.step(nc.vector.tensor_tensor(tmp, r, r, ALU.mult))
                dve.wait_ge(steps.sem, k)
                k = steps.step(nc.vector.tensor_tensor(tmp, tmp, vh, ALU.mult))
                dve.wait_ge(steps.sem, k)
                k = steps.step(nc.vector.scalar_tensor_tensor(out=r, in0=tmp, scalar=1.5, in1=r, op0=ALU.add, op1=ALU.mult))
            dve.wait_ge(steps.sem, k)

        def dve_ln(dve, steps, nb):
            for t in range(NC):
                k = steps.step(nc.vector.bn_stats(st[:, t, :], xraw[:, t, :]))
            dve.wait_ge(steps.sem, k)
            k = steps.step(nc.vector.memset(lt, 0.0))
            for t in range(NC):
                k = steps.step(nc.vector.bn_aggr(mv[:, t, :], st[:, t, :]))
            dve.wait_ge(steps.sem, k)
            k = steps.step(nc.vector.tensor_scalar(lv, mv[:, :, 1], EPS, None, ALU.add))
            dve.wait_ge(steps.sem, k)
            rsqrt(dve, steps, lv, lr, lt, lm)
            steps.step(nc.vector.tensor_copy(rstd, lr))
            steps.step(nc.vector.tensor_scalar(rp1, lr, 1.0, None, ALU.add))
            nc.vector.scalar_tensor_tensor(out=nmr, in0=mv[:, :, 0], scalar=-1.0, in1=lr, op0=ALU.mult,
                                           op1=ALU.mult).then_inc(ln_ok.sem, 1)

        def dve_xl(dve, nb):
            for t in range(NC):
                dve.wait_ge(xh_ok.sem, xh_ok.at(nb, t))
                nc.vector.scalar_tensor_tensor(out=xl[:, :, t * P:(t + 1) * P], in0=bank(6 + t % 2).rearrange("p (k n) -> p k n", k=KD),
                                               scalar=XS, in1=xh[:, :, t * P:(t + 1) * P], op0=ALU.mult,
                                               op1=ALU.subtract).then_inc(xl_ok.sem, 1)

        def heads(v):
            return v.rearrange("p (c h) -> p c h", c=NC)

        def dve_dt(dve, steps, nb):
            dve.wait_ge(pe_dt.sem, pe_dt.at(nb, 0))
            nc.vector.scalar_tensor_tensor(out=heads(dr), in0=heads(bank(6)[:, 0:W4]), scalar=f_in[:, 0:1],
                                           in1=dtb[:].unsqueeze(1).to_broadcast([P, NC, NH]), op0=ALU.mult,
                                           op1=ALU.add).then_inc(dt_raw.sem, 1)
            dve.wait_ge(dt_exp.sem, dt_exp.at(nb, 0))
            nc.vector.tensor_scalar(du, de, 1.0, None, ALU.add).then_inc(dt_u.sem, 1)
            dve.wait_ge(dt_u.sem, dt_u.at(nb, 0))
            k = steps.step(nc.vector.scalar_tensor_tensor(out=de, in0=du, scalar=-1.0, in1=de, op0=ALU.add, op1=ALU.subtract))
            k = steps.step(nc.vector.reciprocal(dm, du))
            dve.wait_ge(steps.sem, k)
            k = steps.step(nc.vector.tensor_tensor(dm, dm, de, ALU.mult))
            dve.wait_ge(dt_ln.sem, dt_ln.at(nb, 0))
            k2 = steps.step(nc.vector.scalar_tensor_tensor(out=dl, in0=dr, scalar=0.0, in1=dl, op0=ALU.max, op1=ALU.add))
            dve.wait_ge(steps.sem, k2)
            k = steps.step(nc.vector.tensor_tensor(dtv, dl, dm, ALU.subtract))
            dve.wait_ge(steps.sem, k)
            nc.vector.tensor_tensor(heads(av), heads(dtv), nega[:].unsqueeze(1).to_broadcast([P, NC, NH]),
                                    ALU.mult).then_inc(dt_a.sem, 1)

        @block.vector
        def _(dve):
            steps = Steps(dve_steps, DVE_STEPS)
            dve.wait_ge(d_con, 32)
            steps.step(nc.vector.tensor_scalar(cmean[:], ones, 1.0 / E, None, ALU.mult))
            nc.vector.tensor_copy(ones16, ones).then_inc(ones16_ok, 1)
            dve.wait_ge(d_x0, 16)
            dve_ln(dve, steps, 0)
            dve.wait_ge(alog_e, 1)
            steps.step(nc.vector.tensor_scalar(nega[:], nega[:], -1.0, None, ALU.mult))

            def to_scale(n, sums, op):
                v, q = total[:, n:n + 1], p2[:, n:n + 1]
                k = steps.step(nc.vector.tensor_reduce(out=v, in_=sums, axis=AX.X, op=op))
                dve.wait_ge(steps.sem, k)
                if n == 1:
                    dve.nop().then_inc(w13_read, 1)
                    dve.nop().then_inc(ready, 1)
                k = steps.step(nc.vector.tensor_scalar(q.bitcast(I32), v.bitcast(I32), 1, None, ALU.logical_shift_right))
                dve.wait_ge(steps.sem, k)
                k = steps.step(nc.vector.tensor_scalar(q.bitcast(I32), q.bitcast(I32), 1, 0x1FC00000, ALU.mult, ALU.add))
                dve.wait_ge(steps.sem, k)
                k = steps.step(nc.vector.tensor_scalar(q.bitcast(I32), q.bitcast(I32), 0x7F800000, None, ALU.bitwise_and))
                dve.wait_ge(steps.sem, k)
                k = steps.step(nc.vector.tensor_scalar(q, q, 2.0 ** -20, None, ALU.max))
                dve.wait_ge(steps.sem, k)
                k = steps.step(nc.vector.reciprocal(scl[:, n:n + 1], q))
                steps.step(nc.vector.tensor_scalar(inv[:, n:n + 1], q, 2.0 ** -14, None, ALU.mult))
                dve.wait_ge(steps.sem, k)
                k = steps.step(nc.vector.tensor_scalar(scl[:, n:n + 1], scl[:, n:n + 1], 2.0 ** 14, None, ALU.mult))
                dve.wait_ge(steps.sem, k)

            dve_xl(dve, 0)
            dve.wait_ge(d_w2, 16)
            for n in range(2):
                butterfly(nc.vector, dve, n, 0, D_SPLIT, bf_dve)
            dve.wait_ge(sums_w, 1)
            to_scale(0, bank(3)[:, 0:KD], ALU.add)
            steps.step(nc.vector.tensor_scalar(f_in[:], inv[:, 0:1], 1 / XS, None, ALU.mult))
            k = steps.step(nc.vector.tensor_scalar(f_half[:], inv[:, 0:1], 0.5 / XS, None, ALU.mult))
            dve.wait_ge(steps.sem, k)
            dve.wait_ge(d_par, 16 * N_PAR)
            steps.step(nc.vector.tensor_scalar(cw[:], cw[:], f_half[:, 0:1], None, ALU.mult))
            steps.step(nc.vector.tensor_scalar(cb[:], cb[:], 0.5, None, ALU.mult))
            nc.vector.tensor_scalar(p2[:, 3:4], p2[:, 0:1], 1.0, None, ALU.mult).then_inc(scale_ok, 1)
            dve.wait_ge(wdt_h, 1)
            nc.vector.scalar_tensor_tensor(out=wdt_lo[:], in0=win_raw[:, :, DT:DT + NH], scalar=scl[:, 0:1], in1=wdt_hi[:],
                                           op0=ALU.mult, op1=ALU.subtract).then_inc(wdt_h, 1)
            butterfly(nc.vector, dve, 2, 0, D_SPLIT, bf_dve)
            dve_dt(dve, steps, 0)
            dve.wait_ge(sums_w, 2)
            to_scale(3, bank(2)[:, 0:KD], ALU.add)
            to_scale(2, bank(2)[:, KD:KD + QE], ALU.add)
            steps.step(nc.vector.tensor_scalar(f_out[:], inv[:, 2:3], 1 / XS, None, ALU.mult))
            k = steps.step(nc.vector.tensor_scalar(nws, nw[:], scl[:, 2:3], None, ALU.mult))
            dve.wait_ge(steps.sem, k)
            nc.vector.tensor_scalar(f_had[:], scl[:, 3:4], float(np.float32(1 / np.sqrt(HF))), None, ALU.mult).then_inc(scale_ok, 2)
            butterfly(nc.vector, dve, 3, 0, D_SPLIT, bf_dve)
            for q in range(QE):
                dve.wait_ge(wo_h, q + 1)
                steps.step(nc.vector.scalar_tensor_tensor(out=wo_lo[:, q, :], in0=wo_raw[:, q, :], scalar=nws[:, q:q + 1],
                                                          in1=wo_hi[:, q, :], op0=ALU.mult, op1=ALU.subtract))
            for j in range(JF):
                dve.wait_ge(had_hi, j + 1)
                nc.vector.scalar_tensor_tensor(out=w2p[:, j, D:2 * D], in0=bank(j % 4), scalar=f_had[:, 0:1],
                                               in1=w2p[:, j, 0:D], op0=ALU.mult, op1=ALU.subtract).then_inc(had_lo, 1)

            def split_lo(b, p):
                dve.wait_ge(w_hi.sem, w_hi.at(b, p))
                nc.vector.scalar_tensor_tensor(out=part_lo[p % PARTS], in0=raw[p % RAW], scalar=weight_scale(STREAM[p % NT]),
                                               in1=part_hi[p % PARTS], op0=ALU.mult, op1=ALU.subtract).then_inc(w_lo.sem, 1)

            for p in range(RAW):
                split_lo(0, p)
            dve.wait_ge(w13_sums, KD)
            dve.wait_ge(had_lo, JF)
            to_scale(1, bank(4, 4), ALU.max)
            k = steps.step(nc.vector.tensor_scalar(f_13[:], inv[:, 1:2], 0.5 / XS, None, ALU.mult))
            k = steps.step(nc.vector.tensor_scalar(f_w2[:], inv[:, 1:2], inv[:, 1:2], 1 / HID, ALU.mult, ALU.mult))
            dve.wait_ge(steps.sem, k)
            k = steps.step(nc.vector.tensor_tensor(f_w2[:], f_w2[:], inv[:, 3:4], ALU.mult))
            dve.wait_ge(steps.sem, k)
            nc.vector.tensor_copy(p2[:, 3:4], p2[:, 1:2]).then_inc(w13_scale, 1)
            dve.wait_ge(ready, ENGINES_READY)
            for p in range(RAW, AHEAD):
                split_lo(0, p)
            with dve.Fori(0, NB) as b:
                steps.enter(b)

                def silu_conv(key):
                    dve.wait_ge(tanh_ok.sem, tanh_ok.at(b, TANH[key]))
                    nc.vector.scalar_tensor_tensor(out=XT[:, key[1], :], in0=tb[TANH[key] % 2], scalar=1.0,
                                                   in1=acc[C_ORDER[key[1]] % 2], op0=ALU.add,
                                                   op1=ALU.mult).then_inc(xt_done.sem, 1)

                def finish(key):
                    kind, i = key
                    p = POS[key]
                    src = tile_bank(p)
                    if kind == "C":
                        n = C_ORDER[i]
                        a = acc[n % 2]
                        due = STREAM[p - 2] if p > 1 and STREAM[p - 2][0] == "C" else None
                        if due and C_ORDER[due[1]] == n - 2:
                            silu_conv(due)
                            due = None
                        dve.wait_ge(acc_ok.sem, acc_ok.at(b, n))
                        for s in range(1, TAPS):
                            ins = nc.vector.scalar_tensor_tensor(out=a[:, s:L], in0=src[:, 0:L - s],
                                                                 scalar=cw[:, i, TAPS - 1 - s:TAPS - s], in1=a[:, s:L],
                                                                 op0=ALU.mult, op1=ALU.add)
                            if s < TAPS - 1:
                                k = steps.step(ins)
                                if s == 1 and due:
                                    silu_conv(due)
                                dve.wait_ge(steps.sem, k)
                        ins.then_inc(evac.sem, 1)
                    elif kind == "Z":
                        dve.wait_ge(tanh_ok.sem, tanh_ok.at(b, TANH[key]))
                        nc.vector.scalar_tensor_tensor(out=gz[:, i, :], in0=tb[TANH[key] % 2], scalar=1.0, in1=src,
                                                       op0=ALU.add, op1=ALU.mult).then_inc(evac.sem, 1)
                    elif kind == "A":
                        dve.wait_ge(tanh_ok.sem, tanh_ok.at(b, TANH[key]))
                        dve.wait_ge(hid_l.sem, hid_l.at(b, max(i - 2, -1)))
                        nc.vector.scalar_tensor_tensor(out=hs[i % 2], in0=tb[TANH[key] % 2], scalar=1.0, in1=src,
                                                       op0=ALU.add, op1=ALU.mult).then_inc(evac.sem, 1)
                    else:
                        dve.wait_ge(tile_done.sem, tile_done.at(b, p))
                        dve.wait_ge(evac.sem, evac.at(b, p - 1))
                        nc.vector.scalar_tensor_tensor(out=hs[i % 2], in0=src, scalar=HID / (2 * XS * XS), in1=hs[i % 2],
                                                       op0=ALU.mult, op1=ALU.mult).then_inc(evac.sem, 1)

                k = steps.step(nc.vector.tensor_copy(rp1_cur, rp1))
                k = steps.step(nc.vector.tensor_copy(nmr_cur, nmr))
                for kind, i in SCHEDULE:
                    c = i
                    if kind in "CZAU":
                        split_lo(b, POS[kind, i] + AHEAD)
                        finish((kind, i))
                        p = POS[kind, i]
                        if kind != "C" and p > 1 and STREAM[p - 2][0] == "C":
                            silu_conv(STREAM[p - 2])
                    elif kind == "T":
                        dve.wait_ge(pe_x.sem, pe_x.at(b, c))
                        nc.vector.tensor_tensor(Xdt.rearrange("p (h d) -> p h d", h=NH),
                                                bank(4, 2).rearrange("p (h d) -> p h d", h=NH),
                                                dtv[:, c * NH:(c + 1) * NH].unsqueeze(2).to_broadcast([P, NH, HD]),
                                                ALU.mult).then_inc(xdt_ok.sem, 1)
                        dve.wait_ge(pe_g.sem, pe_g.at(b, c))
                        nc.vector.tensor_tensor(Gm, bank(7)[:, 0:P], tri_le, ALU.mult).then_inc(gm_ok.sem, 1)
                    elif kind == "X":
                        dve.wait_ge(eexp_ok.sem, eexp_ok.at(b, c))
                        dve.wait_ge(gm_ok.sem, gm_ok.at(b, c))
                        nc.vector.tensor_tensor(Eb, Eb, Gm.unsqueeze(1).to_broadcast([P, NH, P]), ALU.mult).then_inc(m_ok.sem, 1)
                    elif kind == "S":
                        if c > 0:
                            dve.wait_ge(pe_off.sem, pe_off.at(b, c - 1))
                            dve.wait_ge(d_ecsb, (b * (NC - 1) + c) * 32)
                            nc.vector.tensor_tensor(t1, bank(6, 2), ecsb, ALU.mult).then_inc(t1_ok.sem, 1)
                    elif kind == "R":
                        if 0 < c < NC - 1:
                            dve.wait_ge(pe_state.sem, pe_state.at(b, c))
                            dve.wait_ge(sdec_ok.sem, sdec_ok.at(b, c - 1))
                            nc.vector.tensor_tensor(state, bank(4, 2), state, ALU.add).then_inc(state_ok.sem, 1)
                    elif kind == "Y":
                        dve.wait_ge(pe_diag.sem, pe_diag.at(b, c))
                        if c > 0:
                            dve.wait_ge(t2_ok.sem, t2_ok.at(b, c - 1))
                        else:
                            dve.wait_ge(xd_ok.sem, xd_ok.at(b, c))
                        nc.vector.tensor_tensor(y, bank(6, 2), XD, ALU.add).then_inc(diag_read.sem, 1)
                        dve.wait_ge(diag_read.sem, diag_read.at(b, c))
                        y3 = y.rearrange("p (q l) -> p q l", q=QE)
                        nc.vector.scalar_tensor_tensor(out=y3, in0=y3, scalar=f_half[:, 0:1], in1=gz[:, :, c * P:(c + 1) * P],
                                                       op0=ALU.mult, op1=ALU.mult).then_inc(ygate_ok.sem, 1)
                    elif kind == "Q":
                        dve.wait_ge(sq_ok.sem, sq_ok.at(b, c))
                        nc.vector.tensor_reduce(out=sqr, in_=t1.rearrange("p (q l) -> p l q", q=QE), axis=AX.X,
                                                op=ALU.add).then_inc(sqr_ok.sem, 1)
                    elif kind == "N":
                        dve.wait_ge(pe_mean.sem, pe_mean.at(b, c))
                        nc.vector.tensor_scalar(nv, out_bank(c)[0][:, 0:P], EPS, None, ALU.add).then_inc(mean_read.sem, 1)
                        dve.wait_ge(mean_read.sem, mean_read.at(b, c))
                        rsqrt(dve, steps, nv, nr, ntmp, sqr)
                        y3 = y.rearrange("p (q l) -> p q l", q=QE)
                        nc.vector.tensor_tensor(y3, y3, nr.unsqueeze(1).to_broadcast([P, QE, P]), ALU.mult).then_inc(yn_ok.sem, 1)
                    elif kind == "V":
                        y3 = y.rearrange("p (q l) -> p q l", q=QE)
                        dve.wait_ge(yh_ok.sem, yh_ok.at(b, c))
                        nc.vector.scalar_tensor_tensor(out=yl, in0=y3, scalar=XS, in1=yh, op0=ALU.mult,
                                                       op1=ALU.subtract).then_inc(yl_ok.sem, 1)
                    elif kind == "W":
                        dve.wait_ge(d_xr[c % 2], (b * (NC // 2) + (c // 2 + 1)) * 16)
                        k = steps.step(nc.vector.tensor_scalar(xr[c % 2], xr[c % 2], rp1_cur[:, c:c + 1], nmr_cur[:, c:c + 1],
                                                               ALU.mult, ALU.add))
                        dve.wait_ge(steps.sem, k)
                        dve.wait_ge(pe_wout.sem, pe_wout.at(b, c))
                        if c == 0:
                            dve.wait_ge(d_out, b * (NC * 16) + 1)
                        nc.vector.scalar_tensor_tensor(out=racc[:, c, :], in0=out_bank(c)[1], scalar=f_out[:, 0:1], in1=xr[c % 2],
                                                       op0=ALU.mult, op1=ALU.add).then_inc(mamba_evac.sem, 1)
                    elif kind == "LN":
                        dve.wait_ge(d_xraw, (b + 1) * 16)
                        dve_ln(dve, steps, b + 1)
                    elif kind == "XT":
                        dve_xl(dve, b + 1)
                    elif kind == "DT":
                        dve_dt(dve, steps, b + 1)
                    elif kind == "OUT":
                        dve.wait_ge(w2_used.sem, w2_used.at(b, JF - 1))
                        dve.wait_ge(mamba_evac.sem, mamba_evac.at(b, NC - 1))
                        for t in range(NC):
                            nc.vector.scalar_tensor_tensor(out=racc[:, t, :], in0=bank(t), scalar=f_w2[:, 0:1],
                                                           in1=racc[:, t, :], op0=ALU.mult, op1=ALU.add).then_inc(ffn_evac.sem, 1)
                steps.leave()

        @block.gpsimd
        def _(pool):
            pool.wait_ge(d_w2, 16)
            for n in range(4):
                butterfly(nc.gpsimd, pool, n, D_SPLIT, D, bf_pool)
            pool.wait_ge(pe_xt.sem, pe_xt.at(0, NC - 1))
            for k in range(KD):
                pool.wait_ge(d_w13[(2 * k + 1) % 4], 16 * ((2 * k + 1) // 4 + 1))
                if k >= 2:
                    pool.wait_ge(w13_sums, k - 1)
                w = w13_raw[(2 * k + 1) % 4]
                nc.gpsimd.tensor_tensor(sq_pool[k % 2], w, w, ALU.mult).then_inc(w13_sq_pool, 1)
            pool.nop().then_inc(ready, 1)
            pool.wait_ge(ready, ENGINES_READY)
            with pool.Fori(0, NB) as b:
                for kind, i in SCHEDULE:
                    c = i
                    if kind == "U":
                        pool.wait_ge(hid_h.sem, hid_h.at(b, i))
                        nc.gpsimd.tensor_tensor(hid_lo[:, i, :], hs[i % 2], hid_hi[:, i, :], ALU.subtract).then_inc(hid_l.sem, 1)
                    elif kind == "E":
                        pool.wait_ge(d_csbc, (b * NC + (c + 1)) * 16)
                        pool.wait_ge(sums_ok.sem, sums_ok.at(b, 0))
                        pool.wait_ge(pe_diag.sem, pe_diag.at(b, c - 1))
                        nc.gpsimd.tensor_tensor(Eb, csbc, cs_s[:, c * NH:(c + 1) * NH].unsqueeze(2).to_broadcast([P, NH, P]),
                                                ALU.subtract).then_inc(esub_ok.sem, 1)
                        pool.wait_ge(esub_ok.sem, esub_ok.at(b, c))
                        nc.gpsimd.tensor_tensor(pool_mark, ones[:, 0:1], ones[:, 0:1], ALU.mult)
                        nc.gpsimd.tensor_scalar(Eb, Eb, 0.0, -3.0e38, ALU.min, ALU.max).then_inc(emin_ok.sem, 1)
                    elif kind == "T":
                        if c < NC - 1:
                            pool.wait_ge(xdt_ok.sem, xdt_ok.at(b, c))
                            nc.gpsimd.tensor_tensor(Xdec.rearrange("p (h d) -> p h d", h=NH), Xdt.rearrange("p (h d) -> p h d", h=NH),
                                                    dec[:, c * NH:(c + 1) * NH].unsqueeze(2).to_broadcast([P, NH, HD]),
                                                    ALU.mult).then_inc(xdec_ok.sem, 1)
                    elif kind == "S" and c > 0:
                        pool.wait_ge(t1_ok.sem, t1_ok.at(b, c - 1))
                        pool.wait_ge(xd_ok.sem, xd_ok.at(b, c))
                        nc.gpsimd.tensor_tensor(XD, XD, t1, ALU.add).then_inc(t2_ok.sem, 1)
                        if c < NC - 1:
                            nc.gpsimd.tensor_tensor(state.rearrange("p (h d) -> p h d", h=NH), state.rearrange("p (h d) -> p h d", h=NH),
                                                    tot[:, c * NH:(c + 1) * NH].unsqueeze(2).to_broadcast([P, NH, HD]),
                                                    ALU.mult).then_inc(sdec_ok.sem, 1)


def constants():
    k = np.arange(P)
    bits = np.array([[bin(a & c).count("1") for c in k] for a in k])
    return np.concatenate([np.eye(P), k[:, None] <= k[None, :], k[:, None] > k[None, :],
                           np.ones((P, P)), 1.0 - 2.0 * (bits % 2)], axis=1).astype(np.float32)


def kernel(L0_attn_x, L0_attn_w_in, L0_attn_conv_w, L0_attn_conv_b, L0_attn_dt_bias, L0_attn_A_log, L0_attn_D,
           L0_attn_norm_w, L0_attn_w_out, L0_ffn_W1, L0_ffn_W2, L0_ffn_W3):
    import concourse.bacc as _bacc
    from concourse.bass_utils import run_bass_kernel_spmd as _run

    x = np.asarray(L0_attn_x)
    con = np.ascontiguousarray
    arrays = {
        "x": con(np.concatenate([x, x[:1]])),
        "w_in": con(L0_attn_w_in),
        "w1t": con(np.asarray(L0_ffn_W1).T),
        "w3t": con(np.asarray(L0_ffn_W3).T),
        "w2t": con(np.asarray(L0_ffn_W2).T),
        "w_out": con(L0_attn_w_out),
        "conv_w": con(np.asarray(L0_attn_conv_w).reshape(MC, P, TAPS).transpose(1, 0, 2)),
        "conv_b": con(np.asarray(L0_attn_conv_b).reshape(MC, P).T),
        "dt_bias": con(np.broadcast_to(np.asarray(L0_attn_dt_bias), (P, NH))),
        "a_log": con(np.broadcast_to(np.asarray(L0_attn_A_log), (P, NH))),
        "d_cols": con(np.repeat(np.asarray(L0_attn_D), HD).reshape(QE, P).T),
        "norm_w": con(np.asarray(L0_attn_norm_w).reshape(QE, P).T),
        "consts": constants(),
    }
    nc = _bacc.Bacc("TRN2", target_bir_lowering=False, num_devices=1)
    args = [nc.dram_tensor(n, a.shape, mybir.dt.from_np(a.dtype), kind="ExternalInput").ap() for n, a in arrays.items()]
    out = nc.dram_tensor("out", (NB, L, D), FP32, kind="ExternalOutput").ap()
    build(nc, *args, out)
    r = _run(nc, [arrays], core_ids=[0])
    return r.results[0]["out"]
```
